# Optimizing a Trainium2 kernel written in Bass

```python
import numpy as np
import jax
import jax.numpy as jnp

def _softmax(x, axis=-1):
    return jax.nn.softmax(x, axis=axis)

def _gelu(x):
    return jax.nn.gelu(x, approximate=True)

def _silu(x):
    return jax.nn.silu(x)

def _sigmoid(x):
    return jax.nn.sigmoid(x)

def _layernorm(x, axis=-1, eps=1e-05):
    m = jnp.mean(x, axis=axis, keepdims=True)
    v = jnp.var(x, axis=axis, keepdims=True)
    return (x - m) / jnp.sqrt(v + eps)

def _scatter_add(tgt, idx, src, axis=0):
    return tgt.at[idx].add(src)

def _segment_sum(src, seg, n):
    return jax.ops.segment_sum(src, seg, n)
kernel_name = 'mk_adj_ffn_d1_adj_r2_0653f6'

def setup_inputs(seed: int=0):
    np.random.seed(seed)
    _w = jnp.asarray

    def _rec_inputs():
        import jax
        import jax.numpy as jnp
        _gk = jax.random.key(seed)
        x = 7.22e-05 + 1 * jax.random.normal(jax.random.fold_in(_gk, 1), (8, 1024, 128), jnp.float32)
        _w = (1.0 + jnp.arange(1024, dtype=jnp.float32)) ** (-0.5)
        _w = _w / _w.mean()
        _pij = jnp.clip(0.0078125 * _w[:, None] * _w[None, :], 0.0, 1.0)
        _a = jax.random.uniform(jax.random.fold_in(_gk, 2), (8, 1024, 1024)) < _pij
        _a = jnp.logical_or(_a, jnp.swapaxes(_a, -1, -2))
        _a = jnp.logical_or(_a, jnp.eye(1024, dtype=bool))
        _af = _a.astype(jnp.float32)
        adj = _af
        return (x, adj)
    x, adj = _rec_inputs()

    def _L0_gnn_setup():
        import jax, jax.numpy as jnp
        import numpy as np
        from jax import lax
        DIM = 128
        EPS = 1e-05

        def _bn(h, g, b, m, v):
            scale = g / jnp.sqrt(v + EPS)
            return h * scale[None, :, None] + (b - m * scale)[None, :, None]

        def _conv1d(h, w, pad):
            return lax.conv_general_dilated(h, w, window_strides=(1,), padding=[(pad, pad)], dimension_numbers=('NCH', 'OIH', 'NCH'))
        key = jax.random.key(seed)
        ks = jax.random.split(key, 16)
        bs, n, d = (16, 1024, DIM)
        s = 0.05
        return {'x': jax.random.normal(ks[0], (bs, n, d), jnp.float32), 'mask': jnp.ones((bs, n, n), jnp.float32), 'w_se': jax.random.normal(ks[1], (3, d), jnp.float32) * s, 'b_se': jnp.zeros((3,), jnp.float32), 'conv1_w': jax.random.normal(ks[2], (d, d, 1), jnp.float32) * s, 'bn1_g': jnp.ones((d,), jnp.float32), 'bn1_b': jnp.zeros((d,), jnp.float32), 'bn1_m': jnp.zeros((d,), jnp.float32), 'bn1_v': jnp.ones((d,), jnp.float32), 'conv2_w': jax.random.normal(ks[3], (d, d, 17), jnp.float32) * s, 'bn2_g': jnp.ones((d,), jnp.float32), 'bn2_b': jnp.zeros((d,), jnp.float32), 'bn2_m': jnp.zeros((d,), jnp.float32), 'bn2_v': jnp.ones((d,), jnp.float32), 'w_msg': jax.random.normal(ks[4], (d, d), jnp.float32) * s, 'b_msg': jnp.zeros((d,), jnp.float32), 'w_ih': jax.random.normal(ks[5], (3 * d, 2 * d), jnp.float32) * s, 'b_ih': jnp.zeros((3 * d,), jnp.float32), 'w_hh': jax.random.normal(ks[6], (3 * d, d), jnp.float32) * s, 'b_hh': jnp.zeros((3 * d,), jnp.float32)}
    _L0_gnn_all = _L0_gnn_setup()
    _L0_gnn_in = {k: v for k, v in _L0_gnn_all.items() if k in ('w_se', 'b_se', 'conv1_w', 'bn1_g', 'bn1_b', 'bn1_m', 'bn1_v', 'conv2_w', 'bn2_g', 'bn2_b', 'bn2_m', 'bn2_v', 'w_msg', 'b_msg', 'w_ih', 'b_ih', 'w_hh', 'b_hh')}
    del _L0_gnn_all

    def _L0_ffn_setup():
        import jax, jax.numpy as jnp
        import numpy as np
        B, S, D = (8, 2048, 128)
        H = 4 * D
        CAPACITY = 0.5
        key = jax.random.key(seed)
        ks = jax.random.split(key, 6)
        x = jax.random.normal(ks[0], (B, S, D), dtype=jnp.float32)
        attention_mask = jnp.zeros((B, 1, 1, S), dtype=jnp.float32)
        wr = jax.random.normal(ks[1], (D, 1), dtype=jnp.float32) * 0.02
        br = jnp.zeros((1,), dtype=jnp.float32)
        w1 = jax.random.normal(ks[2], (D, H), dtype=jnp.float32) * 0.02
        b1 = jnp.zeros((H,), dtype=jnp.float32)
        w2 = jax.random.normal(ks[3], (H, D), dtype=jnp.float32) * 0.02
        b2 = jnp.zeros((D,), dtype=jnp.float32)
        return {'x': x, 'attention_mask': attention_mask, 'wr': wr, 'br': br, 'w1': w1, 'b1': b1, 'w2': w2, 'b2': b2}
    _L0_ffn_all = _L0_ffn_setup()
    _L0_ffn_in = {k: v for k, v in _L0_ffn_all.items() if k in ('attention_mask', 'wr', 'br', 'w1', 'b1', 'w2', 'b2')}
    del _L0_ffn_all
    return {'x': x, 'adj': adj, 'L0_gnn_w_se': _L0_gnn_in['w_se'], 'L0_gnn_b_se': _L0_gnn_in['b_se'], 'L0_gnn_conv1_w': _L0_gnn_in['conv1_w'], 'L0_gnn_bn1_g': _L0_gnn_in['bn1_g'], 'L0_gnn_bn1_b': _L0_gnn_in['bn1_b'], 'L0_gnn_bn1_m': _L0_gnn_in['bn1_m'], 'L0_gnn_bn1_v': _L0_gnn_in['bn1_v'], 'L0_gnn_conv2_w': _L0_gnn_in['conv2_w'], 'L0_gnn_bn2_g': _L0_gnn_in['bn2_g'], 'L0_gnn_bn2_b': _L0_gnn_in['bn2_b'], 'L0_gnn_bn2_m': _L0_gnn_in['bn2_m'], 'L0_gnn_bn2_v': _L0_gnn_in['bn2_v'], 'L0_gnn_w_msg': _L0_gnn_in['w_msg'], 'L0_gnn_b_msg': _L0_gnn_in['b_msg'], 'L0_gnn_w_ih': _L0_gnn_in['w_ih'], 'L0_gnn_b_ih': _L0_gnn_in['b_ih'], 'L0_gnn_w_hh': _L0_gnn_in['w_hh'], 'L0_gnn_b_hh': _L0_gnn_in['b_hh'], 'L0_ffn_attention_mask': _L0_ffn_in['attention_mask'], 'L0_ffn_wr': _L0_ffn_in['wr'], 'L0_ffn_br': _L0_ffn_in['br'], 'L0_ffn_w1': _L0_ffn_in['w1'], 'L0_ffn_b1': _L0_ffn_in['b1'], 'L0_ffn_w2': _L0_ffn_in['w2'], 'L0_ffn_b2': _L0_ffn_in['b2']}

def reference(x, adj, L0_gnn_w_se, L0_gnn_b_se, L0_gnn_conv1_w, L0_gnn_bn1_g, L0_gnn_bn1_b, L0_gnn_bn1_m, L0_gnn_bn1_v, L0_gnn_conv2_w, L0_gnn_bn2_g, L0_gnn_bn2_b, L0_gnn_bn2_m, L0_gnn_bn2_v, L0_gnn_w_msg, L0_gnn_b_msg, L0_gnn_w_ih, L0_gnn_b_ih, L0_gnn_w_hh, L0_gnn_b_hh, L0_ffn_attention_mask, L0_ffn_wr, L0_ffn_br, L0_ffn_w1, L0_ffn_b1, L0_ffn_w2, L0_ffn_b2):
    import jax
    import jax.numpy as jnp

    def _L0_gnn_ref(x, mask, w_se, b_se, conv1_w, bn1_g, bn1_b, bn1_m, bn1_v, conv2_w, bn2_g, bn2_b, bn2_m, bn2_v, w_msg, b_msg, w_ih, b_ih, w_hh, b_hh):
        import jax, jax.numpy as jnp
        import numpy as np
        from jax import lax
        DIM = 128
        EPS = 1e-05

        def _bn(h, g, b, m, v):
            scale = g / jnp.sqrt(v + EPS)
            return h * scale[None, :, None] + (b - m * scale)[None, :, None]

        def _conv1d(h, w, pad):
            return lax.conv_general_dilated(h, w, window_strides=(1,), padding=[(pad, pad)], dimension_numbers=('NCH', 'OIH', 'NCH'))
        d = x.shape[-1]
        xc = jnp.transpose(x, (0, 2, 1))
        h = _bn(_conv1d(xc, conv1_w, 0), bn1_g, bn1_b, bn1_m, bn1_v)
        h = jax.nn.relu(h)
        h = _bn(_conv1d(h, conv2_w, 8), bn2_g, bn2_b, bn2_m, bn2_v)
        x_conv = jnp.transpose(jax.nn.relu(h + xc), (0, 2, 1))
        s = x @ w_se.T + b_se
        sq = jnp.sum(s * s, axis=-1)
        dist = sq[:, :, None] + sq[:, None, :] - 2.0 * jnp.einsum('bnd,bmd->bnm', s, s)
        A = jnp.exp(-dist) * mask
        msg = jax.nn.relu(x @ w_msg.T + b_msg)
        x_nmp = jnp.einsum('bnm,bmd->bnd', A, msg)
        x_in = jnp.concatenate([x_conv, x_nmp], axis=-1)
        gi = x_in @ w_ih.T + b_ih
        gh = x @ w_hh.T + b_hh
        gi_r, gi_z, gi_n = (gi[..., :d], gi[..., d:2 * d], gi[..., 2 * d:])
        gh_r, gh_z, gh_n = (gh[..., :d], gh[..., d:2 * d], gh[..., 2 * d:])
        r = jax.nn.sigmoid(gi_r + gh_r)
        z = jax.nn.sigmoid(gi_z + gh_z)
        nn_ = jnp.tanh(gi_n + r * gh_n)
        return (1.0 - z) * nn_ + z * x

    def _L0_ffn_ref(x, attention_mask, wr, br, w1, b1, w2, b2):
        import jax, jax.numpy as jnp
        import numpy as np
        B, S, D = (8, 2048, 128)
        H = 4 * D
        CAPACITY = 0.5
        b, s, d = x.shape
        weights = (jnp.einsum('bsd,do->bso', x, wr) + br)[..., 0]
        k = max(1, int(CAPACITY * s))
        kk = k - 1 if k > 1 else 1
        _, idx = jax.lax.top_k(weights, k)
        sel_idx = idx[:, :kk]
        sel = jnp.take_along_axis(x, sel_idx[:, :, None], axis=1)
        h = jax.nn.gelu(jnp.einsum('bkd,dh->bkh', sel, w1) + b1)
        y = jnp.einsum('bkh,hd->bkd', h, w2) + b2
        w_sel = jnp.take_along_axis(weights, sel_idx, axis=1)
        y = y * w_sel[..., None]
        batch_idx = jnp.arange(b)[:, None]
        processed = jnp.zeros_like(x).at[batch_idx, sel_idx].set(y)
        return processed + x
    x = x + _L0_gnn_ref(_layernorm(x, axis=-1), adj, L0_gnn_w_se, L0_gnn_b_se, L0_gnn_conv1_w, L0_gnn_bn1_g, L0_gnn_bn1_b, L0_gnn_bn1_m, L0_gnn_bn1_v, L0_gnn_conv2_w, L0_gnn_bn2_g, L0_gnn_bn2_b, L0_gnn_bn2_m, L0_gnn_bn2_v, L0_gnn_w_msg, L0_gnn_b_msg, L0_gnn_w_ih, L0_gnn_b_ih, L0_gnn_w_hh, L0_gnn_b_hh)
    x = x + _L0_ffn_ref(_layernorm(x, axis=-1), L0_ffn_attention_mask, L0_ffn_wr, L0_ffn_br, L0_ffn_w1, L0_ffn_b1, L0_ffn_w2, L0_ffn_b2)
    return x

_drawn_inputs = setup_inputs


def setup_inputs(seed=0):
    import zlib

    import numpy as np

    out = dict(_drawn_inputs(seed))
    spreads = {'L0_gnn_b_se': (0.0, 0.8),
     'L0_gnn_bn1_g': (1.0, 0.6),
     'L0_gnn_bn1_b': (0.0, 0.489),
     'L0_gnn_bn1_m': (0.0, 0.44),
     'L0_gnn_bn1_v': (1.0, 0.6),
     'L0_gnn_bn2_g': (1.0, 0.6),
     'L0_gnn_bn2_b': (0.0, 0.751),
     'L0_gnn_bn2_m': (0.0, 0.687),
     'L0_gnn_bn2_v': (1.0, 0.6),
     'L0_gnn_b_msg': (0.0, 0.1),
     'L0_gnn_b_ih': (0.0, 0.278),
     'L0_gnn_b_hh': (0.0, 0.388),
     'L0_ffn_b1': (0.0, 0.8),
     'L0_ffn_b2': (0.0, 0.8)}
    factors = {'L0_ffn_wr': 8.0, 'L0_ffn_w1': 8.0, 'L0_ffn_w2': 8.0}
    for name, (base, spread) in spreads.items():
        noise = np.random.default_rng([zlib.crc32(name.encode()), seed]).standard_normal(out[name].shape)
        drawn = base * np.exp(spread * noise) if base else spread * noise
        out[name] = jnp.asarray(drawn.astype(out[name].dtype))
    for name, factor in factors.items():
        out[name] = (out[name] * factor).astype(out[name].dtype)
    return out
```

```python
from contextlib import ExitStack

import numpy as np

import concourse.bass as bass
from concourse import mybir

F32 = mybir.dt.float32
F32R = mybir.dt.float32r
BF16 = mybir.dt.bfloat16
ALU = mybir.AluOpType
ACT = mybir.ActivationFunctionType

P = 128
B = 8
N = 1024
T = N // P
D = 128
HALF = 512
NH = N // HALF
TH = HALF // P
K2 = 17
PAD = K2 // 2
HID = 4 * D
HT = HID // D
NU = T * NH
S = 3
EPS = 1e-5
KEEP = N // 2 - 1
NE, NA = 3, 4
LAG = 2

C_ID, C_TRI, C_MASK = 0, P, 2 * P
U_HI, U_LO, U_ONE, V_HI, V_LO, V_ONE = range(6)
N_CONST = 2 * P + 6


def constants():
    c = np.zeros((P, N_CONST), np.float32)
    c[:, C_ID:C_ID + P] = np.eye(P)
    c[:, C_TRI:C_TRI + P] = np.triu(np.ones((P, P)), 1)
    m = c[:, C_MASK:]
    for j in range(2):
        for i in range(S):
            r = S * j + i
            m[0 + r, U_HI] = 1
            m[32 + r, U_LO] = 1
            for q in (0, 32):
                m[q + r, V_HI if j == 0 else V_LO] = -2
            m[64 + r, U_HI if j == 0 else U_LO] = 1
            m[64 + r, V_ONE] = 1
            m[96 + r, U_ONE] = 1
            m[96 + r, V_HI if j == 0 else V_LO] = 1
    return c


def build(nc, x, adj, w_se, b_se, conv1_w, bn1_g, bn1_b, bn1_m, bn1_v, conv2_w, bn2_g, bn2_b, bn2_m,
          bn2_v, w_msg, b_msg, w_ih, b_ih, w_hh, b_hh, wr, br, w1, b1, w2, b2, const, out):
    ctx = ExitStack()
    with ctx:
        def sb(name, shape, dt=F32):
            return ctx.enter_context(nc.sbuf_tensor(name, shape, dt))

        def bank(name):
            return ctx.enter_context(nc.psum_tensor(name, [P, HALF], F32))

        def sem(name):
            return ctx.enter_context(nc.semaphore(name))

        def f32(ap):
            return ap.bitcast(F32)

        cst = sb("cst", [P, N_CONST])
        ident = cst[:, C_ID:C_ID + P]
        tri = cst[:, C_TRI:C_TRI + P]

        def mask(k):
            return cst[:, C_MASK + k:C_MASK + k + 1]

        ones = sb("ones", [P, P], BF16)
        vec = sb("vec", [P, 40])
        (V_G1, V_B1, V_M1, V_V1, V_G2, V_B2, V_M2, V_V2) = range(8)
        V_BIH, V_BHH, V_F1, V_F2, V_BR, V_SC1, V_SC2, V_SH1, V_SH2, V_T1, V_T2, V_GB, V_NHB = (
            8, 11, 14, 18, 19, 20, 21, 22, 23, 24, 25, 26, 28)
        V_BSE, V_EXP = 29, 30

        def col(k, n=1):
            return vec[:, k:k + n]

        bmsg = sb("bmsg", [P, D])
        wc1 = sb("wc1", [P, 2, D], F32R)
        wc2 = sb("wc2", [P, 2, K2, D], F32R)
        wmsg = sb("wmsg", [P, 2, D], F32R)
        wse = sb("wse", [P, 2, P], F32R)
        wsf = sb("wsf", [P, P])
        wih = sb("wih", [P, 2, 6, D], F32R)
        whh = sb("whh", [P, 2, 3, D], F32R)
        wf1 = sb("wf1", [P, 2, HID], F32R)
        wf2 = sb("wf2", [P, HT, D])
        wrt = sb("wrt", [P, 2, P], F32R)

        xall = sb("xall", [P, B, T, D])
        adjb = sb("adjb", [P, T, N])
        xn = sb("xn", [P, T, D])
        st = sb("st", [P, T, 6])
        msum, mdif, vsum, mean = (sb(n, [P, T]) for n in ("msum", "mdif", "vsum", "mean"))
        ve = sb("ve", [P, T])
        rstd = sb("rstd", [P, T])
        xT = sb("xT", [P, 2, N])
        xTH = sb("xTH", [P, 2, N], F32R)
        xTL = sb("xTL", [P, 2, N], F32R)
        wk = sb("wk", [P, N])
        hH = sb("hH", [P, N + 2 * PAD], F32R)
        hL = sb("hL", [P, N + 2 * PAD], F32R)
        sH = sb("sH", [P, N], F32R)
        sL = sb("sL", [P, N], F32R)
        U = sb("U", [P, N], F32R)
        V = sb("V", [P, N], F32R)
        xcH = sb("xcH", [P, N], F32R)
        xcL = sb("xcL", [P, N], F32R)
        nmH, nmL = sH, sL
        msg = sb("msg", [P, T, D])
        E = sb("E", [P, NE, HALF])
        A = sb("A", [P, NA, HALF])
        tr = sb("tr", [P, NH, HALF])
        tz = sb("tz", [P, NH, HALF])
        ga = sb("ga", [P, NH, HALF])
        gn = sb("gn", [P, NH, HALF])

        flat = adjb[:, :, :].rearrange("p t n -> p (t n)")
        o = 0

        def stage(n):
            nonlocal o
            o += n
            return flat[:, o - n:o]

        r_c2 = stage(D * K2)
        r_c2s = stage(D * K2)
        r_c1, r_c1s, r_ms = stage(D), stage(D), stage(D)
        r_ih = stage(3 * 2 * D).rearrange("p (g i) -> p g i", g=3)
        r_hh = stage(3 * D).rearrange("p (g i) -> p g i", g=3)
        r_se = stage(D)
        r_w1 = stage(HID)
        r_wr = stage(1)
        g = flat[:, 0:NH * HT * HALF].rearrange("p (h j n) -> p h j n", h=NH, j=HT)
        o = NH * HT * HALF
        W = stage(2 * N).rearrange("p (q n) -> p q n", q=2)
        ws = stage(N)

        D0, D1 = bank("D0"), bank("D1")
        M0, M1 = bank("M0"), bank("M1")
        N0, N1 = bank("N0"), bank("N1")
        C0, C1 = bank("C0"), bank("C1")
        Db, Mb, Nb, Cb = (D0, D1), (M0, M1), (N0, N1), (C0, C1)

        Cmp = sb("Cmp", [P, 2, N], BF16)
        Eq = sb("Eq", [P, 2, P], BF16)
        wcol = sb("wcol", [P, 2, T])

        raw_in, cst_in = sem("raw_in"), sem("cst_in")
        vec_in = sem("vec_in")
        x_in = [sem("x_in0"), sem("x_in1")]
        adj_in = sem("adj_in")
        prep_pool, prep_dve = sem("prep_pool"), sem("prep_dve")
        prep_ps, prep_ev = sem("prep_ps"), sem("prep_ev")
        stats, rstd_ok, xn_ok = sem("stats"), sem("rstd_ok"), sem("xn_ok")
        mom1, mom2, agg = sem("mom1"), sem("mom2"), sem("agg")
        xT_ps, xT_ok, xTH_ok, xTL_ok = sem("xT_ps"), sem("xT_ok"), sem("xTH_ok"), sem("xTL_ok")
        c1_ps, h_ok, hH_ok, hL_ok = sem("c1_ps"), sem("h_ok"), sem("hH_ok"), sem("hL_ok")
        s_ps, s_ok, sH_ok, sL_ok = sem("s_ps"), sem("s_ok"), sem("sH_ok"), sem("sL_ok")
        UV0_ok, UV_ok = sem("UV0_ok"), sem("UV_ok")
        m_ps, mb_ok, msg_ok = sem("m_ps"), sem("mb_ok"), sem("msg_ok")
        c2_ps, pre_ok, xcH_ok, xcL_ok = sem("c2_ps"), sem("pre_ok"), sem("xcH_ok"), sem("xcL_ok")
        d_ps, exp_ok, k_ps, A_ok, nm_ps = (sem("d_ps"), sem("exp_ok"), sem("k_ps"), sem("A_ok"),
                                           sem("nm_ps"))
        nmH_ok, nmL_ok = sem("nmH_ok"), sem("nmL_ok")
        gate_ps = sem("gate_ps")
        tr_ok, tz_ok, ga_ok, gn_ok = sem("tr_ok"), sem("tz_ok"), sem("ga_ok"), sem("gn_ok")
        q1_ok, q2_ok, d_ok, e_ok, o_ok = (sem("q1_ok"), sem("q2_ok"), sem("d_ok"), sem("e_ok"),
                                          sem("o_ok"))
        back_ps, x1_ok = sem("back_ps"), sem("x1_ok")
        t2_ps, t2_ok, t2H_ok, t2L_ok = sem("t2_ps"), sem("t2_ok"), sem("t2H_ok"), sem("t2L_ok")
        xn2_ok, base_ok = sem("xn2_ok"), sem("base_ok")
        w_ps, w_ok, wc_ps, wc_ok = sem("w_ps"), sem("w_ok"), sem("wc_ps"), sem("wc_ok")
        f1_ps, g_ok, y_ps = sem("f1_ps"), sem("g_ok"), sem("y_ps")
        cmp_ok, eq_ok, cnt_ps = sem("cmp_ok"), sem("eq_ok"), sem("cnt_ps")
        ws_ok, ys_ok, fb_ps, fin_ok = sem("ws_ok"), sem("ys_ok"), sem("fb_ps"), sem("fin_ok")
        out_done = sem("out_done")

        def wait(eng, s, b, per, k):
            v = b * per + k
            if not isinstance(v, int) or v > 0:
                eng.wait_ge(s, v)

        block = ctx.enter_context(nc.Block())

        def over_batches(eng, step):
            step(0, 0, True, False)
            with eng.Fori(0, (B - 2) // 2) as pair:
                step(2 * pair + 1, 1, False, False)
                step(2 * pair + 2, 0, False, False)
            step(B - 1, (B - 1) % 2, False, True)

        def tile(h, k):
            return slice(h * HALF + k * P, h * HALF + (k + 1) * P)

        def half(h):
            return slice(h * HALF, (h + 1) * HALF)

        x_v = x.rearrange("b (t p) d -> b p t d", p=P)
        adj_v = adj.rearrange("b (t p) m -> b p t m", p=P)
        out_v = out.rearrange("b (t p) d -> b p t d", p=P)
        N_VEC = 9 + 3 + 2 + 2 * 4 + 1
        N_RAW = 8

        c2s_v = r_c2s.rearrange("p (i k) -> p k i", k=K2)
        PREP = [(r_c1s, wc1)]
        PREP += [(c2s_v[:, k, :], wc2[:, :, k, :]) for k in range(K2)]
        PREP += [(r_ms, wmsg)]
        PREP += [(r_ih[:, gi, part * D:(part + 1) * D], wih[:, :, 2 * gi + part, :])
                 for gi in range(3) for part in range(2)]
        PREP += [(r_hh[:, gi, :], whh[:, :, gi, :]) for gi in range(3)]
        PREP += [(r_se[0:S, :], wsf[:, 0:S])]
        PBANKS = [C0, C1, N0, N1]
        N_PREP = 2 * (len(PREP) - 1) + 1 + 3 + 3 * 2
        N_PARAM = 9
        N_SCALED = N_PARAM + 2

        @block.sync
        def _(sp):
            def load_x(b, q):
                sp.dma_start(xall[:, b, :, :], x_v[b]).then_inc(x_in[q], 16)

            sp.dma_start(cst[:, :], const).then_inc(cst_in, 16)
            load_x(0, 0)
            load_x(1, 1)
            sp.dma_start(r_c1, conv1_w.rearrange("o i k -> o (i k)")).then_inc(raw_in, 16)
            sp.dma_start(r_c2, conv2_w.rearrange("o i k -> o (i k)")).then_inc(raw_in, 16)
            sp.dma_start(r_ms, w_msg).then_inc(raw_in, 16)
            sp.dma_start(r_ih, w_ih.rearrange("(g o) i -> o g i", g=3)).then_inc(raw_in, 16)
            sp.dma_start(r_hh, w_hh.rearrange("(g o) i -> o g i", g=3)).then_inc(raw_in, 16)
            sp.dma_start(r_se[0:S, :], w_se).then_inc(raw_in, 16)
            sp.dma_start(r_w1, w1).then_inc(raw_in, 16)
            sp.dma_start(r_wr, wr).then_inc(raw_in, 16)
            for b in range(2, B):
                sp.wait_ge(x_in[b % 2], 16 * (b // 2))
                load_x(b, b % 2)
                if b == 2:
                    sp.wait_ge(prep_ev, N_PREP)
                    sp.dma_start(adjb[:, :, :], adj_v[0]).then_inc(adj_in, 16)
                else:
                    sp.wait_ge(k_ps, NU * (b - 2))
                    sp.dma_start(adjb[:, :, :], adj_v[b - 2]).then_inc(adj_in, 16)
            for b in range(B - 2, B):
                sp.wait_ge(k_ps, NU * b)
                sp.dma_start(adjb[:, :, :], adj_v[b]).then_inc(adj_in, 16)
            for b in range(B):
                sp.wait_ge(fin_ok, NH * (b + 1))
                sp.dma_start(out_v[b], xall[:, b, :, :]).then_inc(out_done, 16)
            sp.wait_ge(out_done, 16 * B)

        @block.gpsimd
        def _(pool):
            def vload(k, src):
                pool.dma_start(col(k, src.shape[1] if len(src.shape) > 1 else 1)
                               [0:src.shape[0], :], src).then_inc(vec_in, 16)

            nc.gpsimd.memset(vec[:, :], 0.0).then_inc(prep_pool, 1)
            pool.wait_ge(prep_pool, 1)
            for k, v in ((V_G1, bn1_g), (V_B1, bn1_b), (V_M1, bn1_m), (V_V1, bn1_v),
                         (V_G2, bn2_g), (V_B2, bn2_b), (V_M2, bn2_m), (V_V2, bn2_v), (V_F2, b2)):
                vload(k, v.rearrange("(p a) -> p a", a=1))
            with nc.allow_non_contiguous_dma(reason="small parameter vectors"):
                vload(V_BIH, b_ih.rearrange("(g p) -> p g", g=3))
                vload(V_BHH, b_hh.rearrange("(g p) -> p g", g=3))
                vload(V_F1, b1.rearrange("(j p) -> p j", j=HT))
            pool.dma_start(col(V_BR), br.rearrange("(a n) -> a n", a=1).broadcast_to([P, 1])).then_inc(vec_in, 16)
            pool.dma_start(bmsg[:, :], b_msg.rearrange("(a n) -> a n", a=1).broadcast_to([P, D])).then_inc(vec_in, 16)
            for q in range(4):
                for j in range(2):
                    r = 32 * q + S * j
                    pool.dma_start(vec[r:r + S, V_BSE:V_BSE + 1],
                                   b_se.rearrange("(p a) -> p a", a=1)).then_inc(vec_in, 16)
            pool.dma_start(wf2[:, :, :], w2.rearrange("(j p) d -> p j d", p=P)).then_inc(vec_in, 16)
            nc.gpsimd.memset(ones[:, :], 1.0).then_inc(prep_pool, 1)
            nc.gpsimd.memset(col(V_EXP, T), -0.5).then_inc(prep_pool, 1)
            nc.gpsimd.memset(wsf[:, :], 0.0).then_inc(prep_pool, 1)
            pool.wait_ge(vec_in, 16 * N_VEC)
            pool.wait_ge(prep_pool, 4)
            for n, (vv, tt) in enumerate(((V_V1, V_T1), (V_V2, V_T2))):
                nc.gpsimd.tensor_scalar(col(tt), col(vv), EPS, None, ALU.add).then_inc(prep_pool, 1)
                pool.wait_ge(prep_pool, 5 + 2 * n)
                nc.gpsimd.tensor_tensor(col(tt), col(tt), col(V_EXP), ALU.pow).then_inc(prep_pool, 1)

            def inv_std(n):
                wait(pool, agg, n, 1, 1)
                nc.gpsimd.tensor_tensor(rstd[:, :], ve[:, :], col(V_EXP, T), ALU.pow).then_inc(rstd_ok, 1)

            with pool.Fori(0, B) as b:
                inv_std(b)
            with pool.Fori(B, 2 * B) as n:
                inv_std(n)
                wait(pool, xn2_ok, n, 1, 1 - B)
                nc.gpsimd.tensor_tensor(xall[:, n - B, :, :], xall[:, n - B, :, :], xn[:, :, :],
                                        ALU.add).then_inc(base_ok, 1)

        @block.scalar
        def _(act):
            def relu_conv1(b, q):
                for h in range(NH):
                    wait(act, c1_ps, b, NH, h + 1)
                    if h == 0:
                        wait(act, xcL_ok, b - 1, NH, NH)
                    nc.scalar.activation(wk[:, half(h)], Db[h][:, :], ACT.Relu,
                                         bias=col(V_SH1)).then_inc(h_ok, 1)

            def embed(b):
                for h in range(NH):
                    wait(act, s_ps, b, NH, h + 1)
                    wait(act, hL_ok, b, NH, h + 1)
                    nc.scalar.activation(wk[0:64, half(h)], Mb[h][0:64, :], ACT.Identity,
                                         bias=vec[0:64, V_BSE:V_BSE + 1]).then_inc(s_ok, 1)
                    nc.scalar.activation(wk[64:P, half(h)], Mb[h][64:P, :], ACT.Square,
                                         bias=vec[64:P, V_BSE:V_BSE + 1]).then_inc(s_ok, 1)

            def relu_msg(b):
                for h in range(NH):
                    wait(act, mb_ok, b, NH, h + 1)
                    m = msg[:, h * TH:(h + 1) * TH, :]
                    nc.scalar.activation(m, m, ACT.Relu).then_inc(msg_ok, 1)

            def exps(b):
                for u in range(NU):
                    wait(act, d_ps, b, NU, u + 1)
                    wait(act, A_ok, b, NU, u + 1 - NE)
                    nc.scalar.activation(E[:, u % NE, :], Db[u % NH][:, :], ACT.Exp,
                                         scale=-1.0).then_inc(exp_ok, 1)

            def copy_xT(b, q):
                for h in range(NH):
                    wait(act, xT_ps, b, NH, h + 1)
                    if h == 0:
                        wait(act, d_ok, b - 2, NH, NH)
                    nc.scalar.activation(xT[:, q, half(h)], Db[h][:, :], ACT.Copy).then_inc(xT_ok, 1)

            def gates(b, h):
                r, z, nh = (M0, M1, D1) if h == 0 else (C0, C1, N1)
                wait(act, gate_ps, b, 8, 4 * h + 1)
                wait(act, o_ok, b - 1, NH, h + 1)
                nc.scalar.activation(ga[:, h, :], nh[:, :], ACT.Identity, bias=col(V_NHB),
                                     scale=0.5).then_inc(ga_ok, 1)
                wait(act, gate_ps, b, 8, 4 * h + 2)
                nc.scalar.activation(tr[:, h, :], r[:, :], ACT.Tanh, bias=col(V_GB), scale=0.5).then_inc(tr_ok, 1)
                wait(act, gate_ps, b, 8, 4 * h + 3)
                nc.scalar.activation(tz[:, h, :], z[:, :], ACT.Tanh, bias=col(V_GB + 1), scale=0.5).then_inc(tz_ok, 1)

            def candidate(b, h):
                wait(act, q2_ok, b, NH, h + 1)
                wait(act, back_ps, b - 1, NH, NH)
                nc.scalar.activation(gn[:, h, :], ga[:, h, :], ACT.Tanh, bias=col(V_BIH + 2)).then_inc(gn_ok, 1)

            act.wait_ge(prep_dve, N_PARAM)
            copy_xT(0, 0)

            def step(b, q, first, last):
                relu_conv1(b, q)
                if not first:
                    candidate(b - 1, 1)
                embed(b)
                relu_msg(b)
                exps(b)
                if not last:
                    copy_xT(b + 1, 1 - q)
                gates(b, 0)
                candidate(b, 0)
                gates(b, 1)

            over_batches(act, step)
            candidate(B - 1, 1)

            def ffn_head(b, q):
                for h in range(NH):
                    wait(act, t2_ps, b, NH, h + 1)
                    if h == 0:
                        wait(act, t2L_ok, b - 1, NH, NH)
                    nc.scalar.activation(xT[:, 0, half(h)], Db[h][:, :], ACT.Copy).then_inc(t2_ok, 1)
                for h in range(NH):
                    wait(act, w_ps, b, NH, h + 1)
                    if h == 0:
                        wait(act, ws_ok, b - 2, NH, NH)
                    nc.scalar.activation(W[:, q, half(h)], Mb[h][:, :], ACT.Identity,
                                         bias=col(V_BR)).then_inc(w_ok, 1)
                for u in range(NH * HT):
                    h, j = divmod(u, HT)
                    wait(act, f1_ps, b, NH * HT, u + 1)
                    if j == 0:
                        wait(act, y_ps, b - 1, NH, h + 1)
                    nc.scalar.activation(g[:, h, j, :], Cb[u % 2][:, :], ACT.Gelu_apprx_tanh,
                                         bias=col(V_F1 + j)).then_inc(g_ok, 1)

            over_batches(act, lambda b, q, first, last: ffn_head(b, q))

        @block.vector
        def _(dve):
            TS, TT, STT = nc.vector.tensor_scalar, nc.vector.tensor_tensor, nc.vector.scalar_tensor_tensor

            def moments(b, n):
                for t in range(T):
                    nc.vector.bn_stats(st[:, t, :], xall[:, b, t, :]).then_inc(stats, 1)
                (me, mo), (ve_, vo) = ((st[:, :, k], st[:, :, k + 3]) for k in (1, 2))
                wait(dve, stats, n, T, T)
                TT(msum[:, :], me, mo, ALU.add)
                TT(mdif[:, :], me, mo, ALU.subtract)
                TS(vsum[:, :], ve_, 1.0 / D, EPS, ALU.mult, ALU.add).then_inc(mom1, 1)
                wait(dve, mom1, n, 1, 1)
                TS(mean[:, :], msum[:, :], 0.5, None, ALU.mult)
                STT(mdif[:, :], mdif[:, :], 0.25, mdif[:, :], ALU.mult, ALU.mult)
                STT(vsum[:, :], vo, 1.0 / D, vsum[:, :], ALU.mult, ALU.add).then_inc(mom2, 1)
                wait(dve, mom2, n, 1, 1)
                TT(ve[:, :], vsum[:, :], mdif[:, :], ALU.add).then_inc(agg, 1)

            def normalise(b, n, ready):
                wait(dve, rstd_ok, n, 1, 1)
                for t in range(T):
                    i = TS(xn[:, t, :], xall[:, b, t, :], mean[:, t:t + 1], rstd[:, t:t + 1], ALU.subtract, ALU.mult)
                i.then_inc(ready, 1)

            dve.wait_ge(vec_in, 16 * N_VEC)
            dve.wait_ge(prep_pool, 8)
            n_dve = 0

            def small(ins, chained=True):
                nonlocal n_dve
                ins.then_inc(prep_dve, 1)
                n_dve += 1
                if chained:
                    dve.wait_ge(prep_dve, n_dve)

            small(TT(col(V_SC1), col(V_G1), col(V_T1), ALU.mult), False)
            small(TT(col(V_SC2), col(V_G2), col(V_T2), ALU.mult))
            small(TT(col(V_T1), col(V_M1), col(V_SC1), ALU.mult), False)
            small(TT(col(V_T2), col(V_M2), col(V_SC2), ALU.mult))
            small(TT(col(V_SH1), col(V_B1), col(V_T1), ALU.subtract), False)
            small(TT(col(V_SH2), col(V_B2), col(V_T2), ALU.subtract), False)
            small(TT(col(V_GB, 2), col(V_BIH, 2), col(V_BHH, 2), ALU.add))
            small(TS(col(V_GB, 2), col(V_GB, 2), 0.5, None, ALU.mult), False)
            small(TS(col(V_NHB), col(V_BHH + 2), 0.5, None, ALU.mult), False)
            dve.wait_ge(x_in[0], 16)
            moments(0, 0)
            dve.wait_ge(raw_in, 16 * N_RAW)
            small(TS(r_c1s, r_c1, col(V_SC1), None, ALU.mult), False)
            small(TS(r_c2s, r_c2, col(V_SC2), None, ALU.mult), False)
            normalise(0, 0, xn_ok)
            n_ev = 0

            def ev(ins, chained=False):
                nonlocal n_ev
                ins.then_inc(prep_ev, 1)
                n_ev += 1
                if chained:
                    dve.wait_ge(prep_ev, n_ev)

            def split(dst, src):
                ev(nc.vector.tensor_copy(dst[:, 0], src), True)
                ev(TT(dst[:, 1], src, f32(dst[:, 0]), ALU.subtract))

            for n, (src, dst) in enumerate(PREP):
                dve.wait_ge(prep_ps, n + 1)
                ps = PBANKS[n % 4][:, 0:src.shape[0]]
                if n < len(PREP) - 1:
                    split(dst, ps)
                else:
                    ev(nc.vector.tensor_copy(dst, ps), True)
            ev(nc.vector.tensor_copy(wsf[:, S:2 * S], wsf[:, 0:S]), True)
            ev(nc.vector.tensor_copy(wsf[:, 32:64], wsf[:, 0:32]), True)
            ev(nc.vector.tensor_copy(wsf[:, 64:128], wsf[:, 0:64]), True)
            split(wse, wsf[:, :])
            split(wf1, r_w1)
            ev(nc.vector.tensor_copy(wrt[:, 0, :], r_wr.broadcast_to([P, P])), True)
            ev(TT(wrt[:, 1, :], r_wr.broadcast_to([P, P]), f32(wrt[:, 0, :]), ALU.subtract))
            assert n_ev == N_PREP

            def zero_pads():
                for hb in (hH, hL):
                    nc.vector.memset(f32(hb[:, 0:PAD]), 0.0)
                    i = nc.vector.memset(f32(hb[:, PAD + N:]), 0.0)
                i.then_inc(prep_dve, 1)

            zero_pads()
            assert n_dve == N_SCALED

            def split_xT(b, q, ok, okH, okL):
                for h in range(NH):
                    wait(dve, ok, b, NH, h + 1)
                    nc.vector.tensor_copy(xTH[:, q, half(h)], xT[:, q, half(h)]).then_inc(okH, 1)
                    wait(dve, okH, b, NH, h + 1)
                    TT(xTL[:, q, half(h)], xT[:, q, half(h)], f32(xTH[:, q, half(h)]),
                       ALU.subtract).then_inc(okL, 1)

            def split_h(b):
                for h in range(NH):
                    hs = slice(PAD + h * HALF, PAD + (h + 1) * HALF)
                    wait(dve, h_ok, b, NH, h + 1)
                    if h == 0:
                        wait(dve, c2_ps, b - 1, NH, NH)
                    nc.vector.tensor_copy(hH[:, hs], wk[:, half(h)]).then_inc(hH_ok, 1)
                    wait(dve, hH_ok, b, NH, h + 1)
                    TT(hL[:, hs], wk[:, half(h)], f32(hH[:, hs]), ALU.subtract).then_inc(hL_ok, 1)

            def new_gate(b, h):
                ni = D0 if h == 0 else N0
                wait(dve, tr_ok, b, NH, h + 1)
                STT(ga[:, h, :], tr[:, h, :], 1.0, ga[:, h, :], ALU.add, ALU.mult).then_inc(q1_ok, 1)
                wait(dve, q1_ok, b, NH, h + 1)
                wait(dve, gate_ps, b, 8, 4 * h + 4)
                TT(ga[:, h, :], ga[:, h, :], ni[:, :], ALU.add).then_inc(q2_ok, 1)

            def blend(b, h, q):
                wait(dve, gn_ok, b, NH, h + 1)
                TT(ga[:, h, :], xT[:, q, half(h)], gn[:, h, :], ALU.subtract).then_inc(d_ok, 1)
                wait(dve, d_ok, b, NH, h + 1)
                wait(dve, tz_ok, b, NH, h + 1)
                STT(ga[:, h, :], tz[:, h, :], 1.0, ga[:, h, :], ALU.add, ALU.mult).then_inc(e_ok, 1)
                wait(dve, e_ok, b, NH, h + 1)
                STT(gn[:, h, :], ga[:, h, :], 0.5, gn[:, h, :], ALU.mult, ALU.add).then_inc(o_ok, 1)

            def add_msg_bias(b):
                for h in range(NH):
                    wait(dve, m_ps, b, NH, h + 1)
                    if h == 0:
                        wait(dve, nm_ps, b - 1, NU, NU)
                    TT(msg[:, h * TH:(h + 1) * TH, :], Db[h][:, :].rearrange("p (t d) -> p t d", t=TH),
                       bmsg[:, :].unsqueeze(1).broadcast_to([P, TH, D]), ALU.add).then_inc(mb_ok, 1)

            def distance_operands(b):
                for h in range(NH):
                    hs = half(h)
                    wait(dve, s_ok, b, 2 * NH, 2 * h + 2)
                    if h == 0:
                        wait(dve, d_ps, b - 1, NU, NU)
                    nc.vector.tensor_copy(sH[:, hs], wk[:, hs]).then_inc(sH_ok, 1)
                    wait(dve, sH_ok, b, NH, h + 1)
                    TT(sL[:, hs], wk[:, hs], f32(sH[:, hs]), ALU.subtract).then_inc(sL_ok, 1)
                    TS(U[:, hs], f32(sH[:, hs]), mask(U_HI), mask(U_ONE), ALU.mult, ALU.add).then_inc(UV0_ok, 1)
                    TS(V[:, hs], f32(sH[:, hs]), mask(V_HI), mask(V_ONE), ALU.mult, ALU.add).then_inc(UV0_ok, 1)
                    wait(dve, sL_ok, b, NH, h + 1)
                    wait(dve, UV0_ok, b, 2 * NH, 2 * h + 2)
                    STT(U[:, hs], f32(sL[:, hs]), mask(U_LO), f32(U[:, hs]), ALU.mult, ALU.add).then_inc(UV_ok, 1)
                    STT(V[:, hs], f32(sL[:, hs]), mask(V_LO), f32(V[:, hs]), ALU.mult, ALU.add).then_inc(UV_ok, 1)

            def state_to_nodes(b):
                for h in range(NH):
                    wait(dve, back_ps, b, NH, h + 1)
                    xs = xall[:, b, h * TH:(h + 1) * TH, :]
                    TT(xs, xs, Nb[h][:, :].rearrange("p (t d) -> p t d", t=TH), ALU.add).then_inc(x1_ok, 1)

            def conv_out(b, h, q):
                hs = half(h)
                wait(dve, c2_ps, b, NH, h + 1)
                wait(dve, sL_ok, b, NH, NH)
                STT(wk[:, hs], Cb[h][:, :], col(V_SH2), xT[:, q, hs], ALU.add, ALU.add).then_inc(pre_ok, 1)
                wait(dve, pre_ok, b, NH, h + 1)
                TS(xcH[:, hs], wk[:, hs], 0.0, None, ALU.max).then_inc(xcH_ok, 1)
                wait(dve, xcH_ok, b, NH, h + 1)
                STT(xcL[:, hs], wk[:, hs], 0.0, f32(xcH[:, hs]), ALU.max, ALU.subtract).then_inc(xcL_ok, 1)

            def weigh(b, u):
                wait(dve, exp_ok, b, NU, u + 1)
                wait(dve, k_ps, b, NU, u + 1)
                wait(dve, nm_ps, b, NU, u + 1 - NA)
                TT(A[:, u % NA, :], E[:, u % NE, :], Mb[u % NH][:, :], ALU.mult).then_inc(A_ok, 1)

            def split_nmp(b):
                for h in range(NH):
                    wait(dve, nm_ps, b, NU, NU - NH + h + 1)
                    nc.vector.tensor_copy(nmH[:, half(h)], Nb[h][:, :]).then_inc(nmH_ok, 1)
                    wait(dve, nmH_ok, b, NH, h + 1)
                    TT(nmL[:, half(h)], Nb[h][:, :], f32(nmH[:, half(h)]), ALU.subtract).then_inc(nmL_ok, 1)

            split_xT(0, 0, xT_ok, xTH_ok, xTL_ok)

            def step(b, q, first, last):
                split_h(b)
                if not first:
                    new_gate(b - 1, 1)
                add_msg_bias(b)
                if not first:
                    blend(b - 1, 1, 1 - q)
                distance_operands(b)
                if not last:
                    dve.wait_ge(x_in[1 - q], (b + q) * 8 + 16)
                    moments(b + 1, b + 1)
                if not first:
                    state_to_nodes(b - 1)
                if not last:
                    normalise(b + 1, b + 1, xn_ok)
                conv_out(b, 0, q)
                for u in range(NU):
                    weigh(b, u)
                    if u == 1:
                        conv_out(b, 1, q)
                split_nmp(b)
                if not last:
                    split_xT(b + 1, 1 - q, xT_ok, xTH_ok, xTL_ok)
                new_gate(b, 0)
                blend(b, 0, q)

            over_batches(dve, step)
            new_gate(B - 1, 1)
            blend(B - 1, 1, (B - 1) % 2)
            state_to_nodes(B - 1)

            def prepare(b):
                moments(b, b + B)
                if not (isinstance(b, int) and b == 0):
                    wait(dve, base_ok, b - 1, 1, 1)
                    wait(dve, t2_ps, b - 1, NH, NH)
                normalise(b, b + B, xn2_ok)

            def rank_columns(b, q):
                wait(dve, wc_ps, b, 2, 2)
                for h in range(NH):
                    i = nc.vector.tensor_copy(wcol[:, q, h * TH:(h + 1) * TH], Db[h][:, :]
                                              .rearrange("p (t c) -> p t c", t=TH)[:, :, 0])
                i.then_inc(wc_ok, 1)
                wait(dve, wc_ok, b, 1, 1)

            def compare(b, q, t):
                w = wcol[:, q, t:t + 1]
                wait(dve, cnt_ps, b, T, t + 1 - 2)
                i = TS(Cmp[:, t % 2, 0:(t + 1) * P], W[:, q, 0:(t + 1) * P], w, None, ALU.is_lt)
                if t < T - 1:
                    i = TS(Cmp[:, t % 2, (t + 1) * P:], W[:, q, (t + 1) * P:], w, None, ALU.is_le)
                STT(Eq[:, t % 2, :], W[:, q, t * P:(t + 1) * P], w, tri, ALU.is_equal, ALU.mult).then_inc(cmp_ok, 1)

            def select(b, q):
                for h in range(NH):
                    hs = half(h)
                    wait(dve, cnt_ps, b, T, T)
                    STT(ws[:, hs], Mb[h][:, :], float(KEEP), W[:, q, hs], ALU.is_lt, ALU.mult).then_inc(ws_ok, 1)
                    wait(dve, ws_ok, b, NH, h + 1)
                    wait(dve, y_ps, b, NH, h + 1)
                    STT(gn[:, h, :], Nb[h][:, :], col(V_F2), ws[:, hs], ALU.add, ALU.mult).then_inc(ys_ok, 1)

            def finish(b):
                for h in range(NH):
                    wait(dve, fb_ps, b, NH, h + 1)
                    wait(dve, base_ok, b, 1, 1)
                    xs = xall[:, b, h * TH:(h + 1) * TH, :]
                    TT(xs, xs, Db[h][:, :].rearrange("p (t d) -> p t d", t=TH), ALU.add).then_inc(fin_ok, 1)

            prepare(0)

            def ffn_step(b, q, first, last):
                split_xT(b, 0, t2_ok, t2H_ok, t2L_ok)
                if not first:
                    select(b - 1, 1 - q)
                if not last:
                    prepare(b + 1)
                if not first:
                    finish(b - 1)
                rank_columns(b, q)
                for t in range(T):
                    compare(b, q, t)

            over_batches(dve, ffn_step)
            select(B - 1, (B - 1) % 2)
            finish(B - 1)

        @block.tensor
        def _(pe):
            MM, TR = nc.tensor.matmul, nc.tensor.transpose

            def three(out_, wgt, hi, lo, start, stop):
                MM(out_, wgt(0), hi, start=start, stop=False)
                MM(out_, wgt(0), lo, start=False, stop=False)
                return MM(out_, wgt(1), hi, start=False, stop=stop)

            pe.wait_ge(cst_in, 16)
            pe.wait_ge(prep_dve, N_SCALED)
            for n, (src, dst) in enumerate(PREP):
                if n >= 4:
                    m = n - 4
                    pe.wait_ge(prep_ev, 2 * m + 2)
                k = src.shape[0]
                TR(PBANKS[n % 4][:, 0:k], src, ident[0:k, 0:k]).then_inc(prep_ps, 1)

            def nodes_to_features(b, s):
                for h in range(NH):
                    for k in range(TH):
                        i = TR(Db[h][:, k * P:(k + 1) * P], xn[:, h * TH + k, :], ident)
                    i.then_inc(s, 1)

            def conv1(b, q):
                wait(pe, xTL_ok, b, NH, NH)
                wait(pe, q2_ok, b - 1, NH, 1)
                for h in range(NH):
                    three(Db[h][:, :], lambda k: wc1[:, k, :], xTH[:, q, half(h)], xTL[:, q, half(h)],
                          True, True).then_inc(c1_ps, 1)

            def embedding(b, q):
                wait(pe, tz_ok, b - 1, NH, 1)
                for h in range(NH):
                    three(Mb[h][:, :], lambda k: wse[:, k, :], xTH[:, q, half(h)], xTL[:, q, half(h)],
                          True, True).then_inc(s_ps, 1)

            def messages(b, q):
                for h in range(NH):
                    wait(pe, h_ok, b, NH, h + 1)
                    for k in range(TH):
                        o_ = Db[h][:, k * P:(k + 1) * P]
                        xh, xl = xTH[:, q, tile(h, k)], xTL[:, q, tile(h, k)]
                        MM(o_, xh, wmsg[:, 0, :], start=True, stop=False)
                        MM(o_, xh, wmsg[:, 1, :], start=False, stop=False)
                        i = MM(o_, xl, wmsg[:, 0, :], start=False, stop=True)
                    i.then_inc(m_ps, 1)

            def conv2(b, h):
                wait(pe, hL_ok, b, NH, NH)
                if h == 0:
                    wait(pe, tz_ok, b - 1, NH, 2)
                for k in range(K2):
                    a = slice(h * HALF + k, h * HALF + k + HALF)
                    i = three(Cb[h][:, :], lambda w: wc2[:, w, k, :], hH[:, a], hL[:, a], k == 0, k == K2 - 1)
                i.then_inc(c2_ps, 1)

            def state_back(b):
                for h in range(NH):
                    wait(pe, o_ok, b, NH, NH)
                    for k in range(TH):
                        i = TR(Nb[h][:, k * P:(k + 1) * P], gn[:, h, k * P:(k + 1) * P], ident)
                    i.then_inc(back_ps, 1)

            def adjacency(b):
                wait(pe, UV_ok, b, 2 * NH, 2 * NH)
                wait(pe, adj_in, b, 16, 16)
                wait(pe, msg_ok, b, NH, NH)
                wait(pe, mb_ok, b, NH, NH)
                wait(pe, s_ok, b, 2 * NH, 2 * NH)
                wait(pe, x1_ok, b - 1, NH, NH)
                for u in range(NU + LAG):
                    if u < NU:
                        t, h = divmod(u, NH)
                        wait(pe, exp_ok, b, NU, u + 1 - NH) if u >= NH else None
                        MM(Db[h][:, :], U[:, t * P:(t + 1) * P], V[:, half(h)], start=True, stop=True)\
                            .then_inc(d_ps, 1)
                        wait(pe, A_ok, b, NU, u + 1 - NH) if u >= NH else None
                        for k in range(TH):
                            i = TR(Mb[h][:, k * P:(k + 1) * P], adjb[:, h * TH + k, t * P:(t + 1) * P], ident)
                        i.then_inc(k_ps, 1)
                    v = u - LAG
                    if v >= 0:
                        t, h = divmod(v, NH)
                        wait(pe, A_ok, b, NU, v + 1)
                        MM(Nb[h][:, :], msg[:, t, :], A[:, v % NA, :], start=(t == 0), stop=(t == T - 1))\
                            .then_inc(nm_ps, 1)

            def gru(b, h, q):
                r, z, ni, nh = (M0, M1, D0, D1) if h == 0 else (C0, C1, N0, N1)
                hs = half(h)
                X = (xTH[:, q, hs], xTL[:, q, hs])
                XC = (xcH[:, hs], xcL[:, hs])
                NM = (nmH[:, hs], nmL[:, hs])

                def wi(gate, part):
                    return lambda k: wih[:, k, 2 * gate + part, :]

                def wh(gate):
                    return lambda k: whh[:, k, gate, :]

                if h == 0:
                    wait(pe, A_ok, b, NU, NU)
                wait(pe, xcL_ok, b, NH, NH)
                three(r[:, :], wh(0), *X, True, False)
                three(r[:, :], wi(0, 0), *XC, False, False)
                three(z[:, :], wh(1), *X, True, False)
                three(z[:, :], wi(1, 0), *XC, False, False)
                return r, z, ni, nh, X, XC, NM, wi, wh

            def gru_rest(b, h, q, parts, last):
                r, z, ni, nh, X, XC, NM, wi, wh = parts
                if h == 0:
                    if not last:
                        wait(pe, xT_ok, b + 1, NH, NH)
                    else:
                        wait(pe, exp_ok, b, NU, NU)
                else:
                    wait(pe, nmL_ok, b, NH, NH)
                three(nh[:, :], wh(2), *X, True, True).then_inc(gate_ps, 1)
                three(ni[:, :], wi(2, 0), *XC, True, False)
                wait(pe, nmL_ok, b, NH, h + 1)
                three(r[:, :], wi(0, 1), *NM, False, True).then_inc(gate_ps, 1)
                three(z[:, :], wi(1, 1), *NM, False, True).then_inc(gate_ps, 1)
                three(ni[:, :], wi(2, 1), *NM, False, True).then_inc(gate_ps, 1)

            pe.wait_ge(xn_ok, 1)
            nodes_to_features(0, xT_ps)
            pe.wait_ge(prep_ev, N_PREP)

            def step(b, q, first, last):
                conv1(b, q)
                embedding(b, q)
                messages(b, q)
                conv2(b, 0)
                if not first:
                    state_back(b - 1)
                conv2(b, 1)
                adjacency(b)
                if not last:
                    wait(pe, xn_ok, b + 1, 1, 1)
                    wait(pe, exp_ok, b, NU, NU)
                    nodes_to_features(b + 1, xT_ps)
                for h in range(NH):
                    gru_rest(b, h, q, gru(b, h, q), last)

            over_batches(pe, step)
            state_back(B - 1)

            def ffn_up(b, us):
                for u in us:
                    h, j = divmod(u, HT)
                    wait(pe, g_ok, b, NH * HT, u - 1)
                    three(Cb[u % 2][:, :], lambda k: wf1[:, k, j * D:(j + 1) * D], xTH[:, 0, half(h)],
                          xTL[:, 0, half(h)], True, True).then_inc(f1_ps, 1)

            def ffn_down(b, h):
                wait(pe, ys_ok, b - 1, NH, h + 1)
                wait(pe, g_ok, b, NH * HT, (h + 1) * HT)
                for j in range(HT):
                    i = MM(Nb[h][:, :], wf2[:, j, :], g[:, h, j, :], start=(j == 0), stop=(j == HT - 1))
                i.then_inc(y_ps, 1)

            def weight_columns(b, q):
                wait(pe, w_ok, b, NH, NH)
                for h in range(NH):
                    for k in range(TH):
                        i = TR(Db[h][:, k * P:(k + 1) * P], W[:, q, tile(h, k)], ident)
                    i.then_inc(wc_ps, 1)

            def count(b):
                for t in range(T):
                    wait(pe, cmp_ok, b, T, t + 1)
                    if t == 0:
                        wait(pe, w_ok, b, NH, NH)
                    e = t // TH
                    for h in range(NH):
                        MM(Mb[h][:, :], ones[:, :], Cmp[:, t % 2, half(h)], start=(t == 0),
                           stop=(t == T - 1 and h != e))
                    MM(Mb[e][:, (t % TH) * P:(t % TH + 1) * P], ones[:, :], Eq[:, t % 2, :], start=False,
                       stop=(t == T - 1)).then_inc(cnt_ps, 1)

            def update_back(b):
                for h in range(NH):
                    wait(pe, ys_ok, b, NH, h + 1)
                    for k in range(TH):
                        i = TR(Db[h][:, k * P:(k + 1) * P], gn[:, h, k * P:(k + 1) * P], ident)
                    i.then_inc(fb_ps, 1)

            def routing(b, first):
                wait(pe, t2L_ok, b, NH, NH)
                if not first:
                    wait(pe, ws_ok, b - 1, NH, NH)
                for h in range(NH):
                    three(Mb[h][:, :], lambda k: wrt[:, k, :], xTH[:, 0, half(h)], xTL[:, 0, half(h)],
                          True, True).then_inc(w_ps, 1)

            def ffn_step(b, q, first, last):
                wait(pe, xn2_ok, b, 1, 1)
                if not first:
                    wait(pe, wc_ok, b - 1, 1, 1)
                nodes_to_features(b, t2_ps)
                if not first:
                    wait(pe, t2_ok, b, NH, NH)
                    update_back(b - 1)
                routing(b, first)
                ffn_up(b, range(0, HT))
                if not first:
                    wait(pe, fin_ok, b - 1, NH, NH)
                weight_columns(b, q)
                ffn_up(b, range(HT, NH * HT))
                ffn_down(b, 0)
                ffn_down(b, 1)
                count(b)

            pe.wait_ge(gn_ok, NH * B)
            over_batches(pe, ffn_step)
            update_back(B - 1)


_INS = ['x', 'adj', 'L0_gnn_w_se', 'L0_gnn_b_se', 'L0_gnn_conv1_w', 'L0_gnn_bn1_g', 'L0_gnn_bn1_b',
        'L0_gnn_bn1_m', 'L0_gnn_bn1_v', 'L0_gnn_conv2_w', 'L0_gnn_bn2_g', 'L0_gnn_bn2_b',
        'L0_gnn_bn2_m', 'L0_gnn_bn2_v', 'L0_gnn_w_msg', 'L0_gnn_b_msg', 'L0_gnn_w_ih', 'L0_gnn_b_ih',
        'L0_gnn_w_hh', 'L0_gnn_b_hh', 'L0_ffn_wr', 'L0_ffn_br', 'L0_ffn_w1', 'L0_ffn_b1', 'L0_ffn_w2',
        'L0_ffn_b2']


def kernel(**inputs):
    import concourse.bacc as _bacc
    from concourse.bass_utils import run_bass_kernel_spmd as _run

    nc = _bacc.Bacc("TRN2", target_bir_lowering=False, num_devices=1)
    arrays, args = {}, []
    for name in _INS + ["const"]:
        a = constants() if name == "const" else np.ascontiguousarray(inputs[name])
        arrays[f"in_{name}"] = a
        args.append(nc.dram_tensor(f"in_{name}", a.shape, mybir.dt.from_np(a.dtype), kind="ExternalInput").ap())
    args.append(nc.dram_tensor("out_0", (B, N, D), F32, kind="ExternalOutput").ap())
    build(nc, *args)
    r = _run(nc, [arrays], core_ids=[0])
    return r.results[0]["out_0"]
```

```python
from contextlib import ExitStack

import numpy as np

import concourse.bass as bass
from concourse import mybir

F32 = mybir.dt.float32
F32R = mybir.dt.float32r
BF16 = mybir.dt.bfloat16
ALU = mybir.AluOpType
ACT = mybir.ActivationFunctionType

P = 128
B = 8
N = 1024
T = N // P
D = 128
HALF = 512
NH = N // HALF
TH = HALF // P
K2 = 17
PAD = K2 // 2
HID = 4 * D
HT = HID // D
NU = T * NH
S = 3
EPS = 1e-5
KEEP = N // 2 - 1
NE, NA, NS = 2, 4, 3
LAG = 3
NC = 4
ROWS = 32
EARLY = {11: 0, 13: 1, 15: 2}

C_ID, C_TRI, C_MASK = 0, P, 2 * P
U_HI, U_LO, U_ONE, V_HI, V_LO, V_ONE = range(6)
N_CONST = 2 * P + 6


def constants():
    c = np.zeros((P, N_CONST), np.float32)
    c[:, C_ID:C_ID + P] = np.eye(P)
    c[:, C_TRI:C_TRI + P] = np.triu(np.ones((P, P)), 1)
    m = c[:, C_MASK:]
    for j in range(2):
        for i in range(S):
            r = S * j + i
            m[0 + r, U_HI] = 1
            m[32 + r, U_LO] = 1
            for q in (0, 32):
                m[q + r, V_HI if j == 0 else V_LO] = -2
            m[64 + r, U_HI if j == 0 else U_LO] = 1
            m[64 + r, V_ONE] = 1
            m[96 + r, U_ONE] = 1
            m[96 + r, V_HI if j == 0 else V_LO] = 1
    return c


(V_G1, V_B1, V_M1, V_V1, V_G2, V_B2, V_M2, V_V2) = range(8)
V_BIH, V_BHH, V_F1, V_F2, V_BR, V_BSE, V_MSG = 8, 11, 14, 18, 19, 20, 21
N_LOADED = V_MSG + D
V_SC1, V_SC2, V_SH1, V_SH2, V_T1, V_T2, V_GB, V_NHB, V_EXP = (
    N_LOADED + k for k in (0, 1, 2, 3, 4, 5, 6, 8, 9))
N_VEC = V_EXP + T

W_C1, W_SE, W_MSG, W_IH = 0, D, 2 * D, 3 * D
W_HH, W_F1 = W_IH + 6 * D, W_IH + 9 * D
W_F2 = W_F1 + HID
W_R = W_F2 + HID
N_W = W_R + P


def rows_of_embedding(a):
    r = np.zeros((P,) + a.shape[1:], a.dtype)
    for q in range(4):
        for j in range(2):
            r[32 * q + S * j:32 * q + S * (j + 1)] = a
    return r


def lay_out(i):
    g = {k.split("_", 1)[1]: np.asarray(v) for k, v in i.items() if k.startswith("L0_")}
    vecs = [g["gnn_bn1_g"], g["gnn_bn1_b"], g["gnn_bn1_m"], g["gnn_bn1_v"],
            g["gnn_bn2_g"], g["gnn_bn2_b"], g["gnn_bn2_m"], g["gnn_bn2_v"],
            *g["gnn_b_ih"].reshape(3, D), *g["gnn_b_hh"].reshape(3, D),
            *g["ffn_b1"].reshape(HT, D), g["ffn_b2"], np.repeat(g["ffn_br"], P),
            rows_of_embedding(g["gnn_b_se"])]
    vec = np.concatenate([np.stack(vecs, 1), np.tile(g["gnn_b_msg"], (P, 1))], 1)
    ih = g["gnn_w_ih"].reshape(3, D, 2, D).transpose(3, 0, 2, 1).reshape(D, 6 * D)
    hh = g["gnn_w_hh"].reshape(3, D, D).transpose(2, 0, 1).reshape(D, 3 * D)
    f2 = g["ffn_w2"].reshape(HT, P, D).transpose(1, 0, 2).reshape(P, HT * D)
    wall = np.concatenate([g["gnn_conv1_w"][:, :, 0].T, rows_of_embedding(g["gnn_w_se"]).T,
                           g["gnn_w_msg"].T, ih, hh, g["ffn_w1"], f2,
                           np.tile(g["ffn_wr"], (1, P))], 1)
    conv2 = g["gnn_conv2_w"].transpose(1, 2, 0).reshape(D, K2 * D)
    return vec, wall, conv2


def build(nc, x, adj, vectors, weights, conv2_w, const, out):
    ctx = ExitStack()
    with ctx:
        def sb(name, shape, dt=F32):
            return ctx.enter_context(nc.sbuf_tensor(name, shape, dt))

        def bank(name):
            return ctx.enter_context(nc.psum_tensor(name, [P, HALF], F32))

        def sem(name):
            return ctx.enter_context(nc.semaphore(name))

        def f32(ap):
            return ap.bitcast(F32)

        cst = sb("cst", [P, N_CONST])
        ident = cst[:, C_ID:C_ID + P]
        tri = cst[:, C_TRI:C_TRI + P]

        def mask(k):
            return cst[:, C_MASK + k:C_MASK + k + 1]

        ones = sb("ones", [P, P], BF16)
        vec = sb("vec", [P, N_VEC])
        def col(k, n=1):
            return vec[:, k:k + n]

        bmsg = col(V_MSG, D)
        wall = sb("wall", [P, 2, N_W], F32R)
        wc2 = sb("wc2", [P, 2, K2 * D], F32R)

        def weight(at):
            return lambda k: wall[:, k, at:at + D]

        xall = sb("xall", [P, B, T, D])
        adjb = sb("adjb", [P, T, N])
        xn = sb("xn", [P, T, D])
        st = sb("st", [P, T, 6])
        msum, mdif, vsum, mean = (sb(n, [P, T]) for n in ("msum", "mdif", "vsum", "mean"))
        ve = sb("ve", [P, T])
        rstd = sb("rstd", [P, T])
        ve2 = sb("ve2", [P, T])
        mean2, rstd2 = sb("mean2", [P, B, T]), sb("rstd2", [P, B, T])
        xT = sb("xT", [P, 2, N])
        xTH = sb("xTH", [P, 2, N], F32R)
        xTL = sb("xTL", [P, 2, N], F32R)
        wk = sb("wk", [P, N])
        hH = sb("hH", [P, N + 2 * PAD], F32R)
        hL = sb("hL", [P, N + 2 * PAD], F32R)
        sH = sb("sH", [P, N], F32R)
        sL = sb("sL", [P, N], F32R)
        U = sb("U", [P, N], F32R)
        V = sb("V", [P, N], F32R)
        xcH = sb("xcH", [P, N], F32R)
        xcL = sb("xcL", [P, N], F32R)
        nmH, nmL = sH, sL
        msgH = sb("msgH", [P, T, D], F32R)
        msgL = sb("msgL", [P, T, D], F32R)
        AH = sb("AH", [P, NS, HALF], F32R)
        AL = sb("AL", [P, NS, HALF], F32R)
        tr = sb("tr", [P, NH, HALF])
        tz = sb("tz", [P, NH, HALF])
        ga = sb("ga", [P, NH, HALF])
        gn = sb("gn", [P, NH, HALF])

        E = tr
        msg = tr[:, :, :].rearrange("p h (t d) -> p (h t) d", d=D)
        A = [tz[:, 0, :], tz[:, 1, :], ga[:, 0, :], ga[:, 1, :]]

        flat = adjb[:, :, :].rearrange("p t n -> p (t n)")
        raw_w, raw_c2 = flat[:, 0:N_W], flat[:, N_W:N_W + K2 * D]
        g = flat[:, 0:NH * HT * HALF].rearrange("p (h j n) -> p h j n", h=NH, j=HT)
        o = NH * HT * HALF
        W = flat[:, o:o + 2 * N].rearrange("p (q n) -> p q n", q=2)
        ws = flat[:, o + 2 * N:o + 3 * N]
        gH = [[t[:, half_] for t in (a, c) for half_ in (slice(0, HALF), slice(HALF, N))]
              for a, c in ((U, V), (xcH, xcL))]
        gL = [[t[:, half_] for t in (a, c) for half_ in (slice(0, HALF), slice(HALF, N))]
              for a, c in ((sH, sL), (hH, hL))]

        N_PARAM = 9

        D0, D1 = bank("D0"), bank("D1")
        M0, M1 = bank("M0"), bank("M1")
        N0, N1 = bank("N0"), bank("N1")
        C0, C1 = bank("C0"), bank("C1")
        Db, Mb, Nb, Cb = (D0, D1), (M0, M1), (N0, N1), (C0, C1)

        Cmp = [t[:, k, :].bitcast(BF16) for t in (tr, tz) for k in range(2)]
        Eq = [ga[:, 0, k * P // 2:(k + 1) * P // 2].bitcast(BF16) for k in range(NC)]
        wcol = sb("wcol", [P, 2, T])

        w_in, c2_in, cst_in = sem("w_in"), sem("c2_in"), sem("cst_in")
        vec_in = sem("vec_in")
        x_in = [sem("x_in0"), sem("x_in1")]
        x0_in = sem("x0_in")
        adj_in = sem("adj_in")
        prep_pool, prep_dve = sem("prep_pool"), sem("prep_dve")
        wH_ok, wL_ok = sem("wH_ok"), sem("wL_ok")
        stats1, rstd_ok, xn_ok = sem("stats1"), sem("rstd_ok"), sem("xn_ok")
        mom1, mom2, agg = sem("mom1"), sem("mom2"), sem("agg")
        xT_ps, xT_ok, xTH_ok, xTL_ok = sem("xT_ps"), sem("xT_ok"), sem("xTH_ok"), sem("xTL_ok")
        c1_ps, h_ok, hH_ok, hL_ok = sem("c1_ps"), sem("h_ok"), sem("hH_ok"), sem("hL_ok")
        s_ps, s_ok, sH_ok, sL_ok = sem("s_ps"), sem("s_ok"), sem("sH_ok"), sem("sL_ok")
        UV0_ok, UV_ok = sem("UV0_ok"), sem("UV_ok")
        m_ps, mb_ok, msg_ok, msgH_ok, msgL_ok = (sem("m_ps"), sem("mb_ok"), sem("msg_ok"),
                                                 sem("msgH_ok"), sem("msgL_ok"))
        AH_ok, AL_ok, c2_ok = sem("AH_ok"), sem("AL_ok"), sem("c2_ok")
        st2, mo21, mo22, agg2, rstd2_ok = (sem("st2"), sem("mo21"), sem("mo22"), sem("agg2"),
                                           sem("rstd2_ok"))
        gH_ok, gL_ok = sem("gH_ok"), sem("gL_ok")
        c2_ps, pre_ok, xcH_ok, xcL_ok = sem("c2_ps"), sem("pre_ok"), sem("xcH_ok"), sem("xcL_ok")
        d_ps, exp_ok, k_ps, A_ok, nm_ps = (sem("d_ps"), sem("exp_ok"), sem("k_ps"), sem("A_ok"),
                                           sem("nm_ps"))
        nmH_ok, nmL_ok = sem("nmH_ok"), sem("nmL_ok")
        gate_ps = sem("gate_ps")
        tr_ok, tz_ok, ga_ok, gn_ok = sem("tr_ok"), sem("tz_ok"), sem("ga_ok"), sem("gn_ok")
        q1_ok, q2_ok, d_ok, e_ok, o_ok = (sem("q1_ok"), sem("q2_ok"), sem("d_ok"), sem("e_ok"),
                                          sem("o_ok"))
        back_ps, x1_ok = sem("back_ps"), sem("x1_ok")
        t2_ps, t2H_ok, t2L_ok = sem("t2_ps"), sem("t2H_ok"), sem("t2L_ok")
        xn2_ok, base_ok = sem("xn2_ok"), sem("base_ok")
        w_ps, w_ok, wc_ps, wc_ok = sem("w_ps"), sem("w_ok"), sem("wc_ps"), sem("wc_ok")
        f1_ps, g_ok, y_ps = sem("f1_ps"), sem("g_ok"), sem("y_ps")
        cmp_ok, cnt_ps = sem("cmp_ok"), sem("cnt_ps")
        ws_ok, ys_ok, fb_ps, fin_ok = sem("ws_ok"), sem("ys_ok"), sem("fb_ps"), sem("fin_ok")
        out_done = sem("out_done")

        def wait(eng, s, b, per, k):
            v = b * per + k
            if not isinstance(v, int) or v > 0:
                eng.wait_ge(s, v)

        def up_bank(u, first):
            return (Mb if first and u < 2 else Cb)[u % 2]

        block = ctx.enter_context(nc.Block())

        def over_batches(eng, step):
            step(0, 0, True, False)
            with eng.Fori(0, (B - 2) // 2) as pair:
                step(2 * pair + 1, 1, False, False)
                step(2 * pair + 2, 0, False, False)
            step(B - 1, (B - 1) % 2, False, True)

        def tile(h, k):
            return slice(h * HALF + k * P, h * HALF + (k + 1) * P)

        def half(h):
            return slice(h * HALF, (h + 1) * HALF)

        x_v = x.rearrange("b (t p) d -> b p t d", p=P)
        adj_v = adj.rearrange("b (t p) m -> b p t m", p=P)
        out_v = out.rearrange("b (t p) d -> b p t d", p=P)
        PIECES = [(raw_w[:, 0:W_IH], wall[:, :, 0:W_IH]), (raw_c2, wc2[:, :, :]),
                  (raw_w[:, W_IH:], wall[:, :, W_IH:])]

        @block.sync
        def _(sp):
            def load_x(b, q):
                sp.dma_start(xall[:, b, :, :], x_v[b]).then_inc(x_in[q], 16)

            for h, landed in ((0, x0_in), (1, x_in[0])):
                hs = slice(h * TH, (h + 1) * TH)
                sp.dma_start(xall[:, 0, hs, :], x_v[0][:, hs]).then_inc(landed, 16)
            sp.dma_start(cst[:, :], const).then_inc(cst_in, 16)
            sp.dma_start(vec[:, 0:N_LOADED], vectors).then_inc(vec_in, 16)
            sp.dma_start(raw_w, weights).then_inc(w_in, 16)
            sp.dma_start(raw_c2, conv2_w).then_inc(c2_in, 16)
            load_x(1, 1)
            for b in range(2, B):
                sp.wait_ge(x_in[b % 2], 16 * (b // 2))
                load_x(b, b % 2)
                if b == 2:
                    sp.wait_ge(wL_ok, len(PIECES))
                    sp.dma_start(adjb[:, :, :], adj_v[0]).then_inc(adj_in, 16)
                else:
                    sp.wait_ge(k_ps, NU * (b - 2))
                    sp.dma_start(adjb[:, :, :], adj_v[b - 2]).then_inc(adj_in, 16)
            for b in range(B - 2, B):
                sp.wait_ge(k_ps, NU * b)
                sp.dma_start(adjb[:, :, :], adj_v[b]).then_inc(adj_in, 16)
            for b in range(B - 1):
                sp.wait_ge(fin_ok, NH * (b + 1))
                sp.dma_start(out_v[b], xall[:, b, :, :]).then_inc(out_done, 16)
            for h in range(NH):
                sp.wait_ge(fin_ok, NH * (B - 1) + h + 1)
                hs = slice(h * TH, (h + 1) * TH)
                sp.dma_start(out_v[B - 1][:, hs], xall[:, B - 1, hs, :]).then_inc(out_done, 16)
            sp.wait_ge(out_done, 16 * (B - 1 + NH))

        @block.gpsimd
        def _(pool):
            nc.gpsimd.memset(col(V_EXP, T), -0.5).then_inc(prep_pool, 1)
            nc.gpsimd.memset(ones[:, :], 1.0).then_inc(prep_pool, 1)
            pool.wait_ge(prep_pool, 2)

            def inv_std(b):
                wait(pool, agg, b, 1, 1)
                nc.gpsimd.tensor_tensor(rstd[:, :], ve[:, :], col(V_EXP, T), ALU.pow).then_inc(rstd_ok, 1)

            def inv_std2(b):
                wait(pool, agg2, b, 1, 1)
                nc.gpsimd.tensor_tensor(rstd2[:, b, :], ve2[:, :], col(V_EXP, T), ALU.pow).then_inc(rstd2_ok, 1)

            inv_std(0)
            pool.wait_ge(vec_in, 16)
            for n, (vv, tt) in enumerate(((V_V1, V_T1), (V_V2, V_T2))):
                nc.gpsimd.tensor_scalar(col(tt), col(vv), EPS, None, ALU.add).then_inc(prep_pool, 1)
                pool.wait_ge(prep_pool, 3 + 2 * n)
                nc.gpsimd.tensor_tensor(col(tt), col(tt), col(V_EXP), ALU.pow).then_inc(prep_pool, 1)

            inv_std(1)
            with pool.Fori(0, B - 2) as b:
                inv_std(b + 2)
                inv_std2(b)
            inv_std2(B - 2)

            def split_g(b, u):
                h, j = divmod(u, HT)
                wait(pool, gH_ok, b, NH * HT, u + 1)
                nc.gpsimd.tensor_tensor(gL[h][j], g[:, h, j, :], f32(gH[h][j]), ALU.subtract).then_inc(gL_ok, 1)

            def ffn_step(b):
                wait(pool, xn2_ok, b, NH, NH)
                nc.gpsimd.tensor_tensor(xall[:, b, :, :], xall[:, b, :, :], xn[:, :, :],
                                        ALU.add).then_inc(base_ok, 1)
                for u in range(NH * HT):
                    split_g(b, u)

            ffn_step(0)
            inv_std2(B - 1)
            with pool.Fori(1, B) as b:
                ffn_step(b)

        @block.scalar
        def _(act):
            def relu_conv1(b, q):
                for h in range(NH):
                    wait(act, c1_ps, b, NH, h + 1)
                    if h == 0:
                        wait(act, xcL_ok, b - 1, NH, NH)
                    nc.scalar.activation(wk[:, half(h)], Db[h][:, :], ACT.Relu, bias=col(V_SH1),
                                         scale=col(V_SC1)).then_inc(h_ok, 1)

            def embed(b):
                for h in range(NH):
                    wait(act, s_ps, b, NH, h + 1)
                    wait(act, hL_ok, b, NH, h + 1)
                    nc.scalar.activation(wk[0:64, half(h)], Mb[h][0:64, :], ACT.Identity,
                                         bias=vec[0:64, V_BSE:V_BSE + 1]).then_inc(s_ok, 1)
                    nc.scalar.activation(wk[64:P, half(h)], Mb[h][64:P, :], ACT.Square,
                                         bias=vec[64:P, V_BSE:V_BSE + 1]).then_inc(s_ok, 1)

            def relu_msg(b):
                for h in range(NH):
                    wait(act, mb_ok, b, NH, h + 1)
                    m = msg[:, h * TH:(h + 1) * TH, :]
                    nc.scalar.activation(m, m, ACT.Relu).then_inc(msg_ok, 1)

            def bn2(b, h):
                wait(act, c2_ps, b, NH, h + 1)
                wait(act, sL_ok, b, NH, NH)
                nc.scalar.activation(wk[:, half(h)], Cb[h][:, :], ACT.Identity, bias=col(V_SH2),
                                     scale=col(V_SC2)).then_inc(c2_ok, 1)

            def exps(b):
                for u in range(NU + 1):
                    if u < NU:
                        wait(act, d_ps, b, NU, u + 1)
                        wait(act, A_ok, b, NU, u + 1 - NE)
                        nc.scalar.activation(E[:, u % NE, :], Db[u % NH][:, :], ACT.Exp,
                                             scale=-1.0).then_inc(exp_ok, 1)
                    if u > 0:
                        v = u - 1
                        wait(act, A_ok, b, NU, v + 1)
                        wait(act, nm_ps, b, NU, v + 1 - NS)
                        nc.scalar.activation(AH[:, v % NS, :], A[v % NA], ACT.Copy).then_inc(AH_ok, 1)

            def copy_xT(b, q):
                for h in range(NH):
                    wait(act, xT_ps, b, NH, h + 1)
                    if h == 0:
                        wait(act, d_ok, b - 2, NH, NH)
                    nc.scalar.activation(xT[:, q, half(h)], Db[h][:, :], ACT.Copy).then_inc(xT_ok, 1)

            def hi_of_x2T(b):
                for h in range(NH):
                    wait(act, t2_ps, b, NH, h + 1)
                    nc.scalar.activation(xTH[:, 0, half(h)], Db[h][:, :], ACT.Copy).then_inc(t2H_ok, 1)

            def gates(b, h):
                r, z, nh = (M0, M1, D1) if h == 0 else (C0, C1, N1)
                wait(act, gate_ps, b, 8, 4 * h + 1)
                wait(act, o_ok, b - 1, NH, h + 1)
                nc.scalar.activation(ga[:, h, :], nh[:, :], ACT.Identity, bias=col(V_NHB),
                                     scale=0.5).then_inc(ga_ok, 1)
                wait(act, gate_ps, b, 8, 4 * h + 2)
                nc.scalar.activation(tr[:, h, :], r[:, :], ACT.Tanh, bias=col(V_GB), scale=0.5).then_inc(tr_ok, 1)
                wait(act, gate_ps, b, 8, 4 * h + 3)
                nc.scalar.activation(tz[:, h, :], z[:, :], ACT.Tanh, bias=col(V_GB + 1), scale=0.5).then_inc(tz_ok, 1)

            def candidate(b, h):
                wait(act, q2_ok, b, NH, h + 1)
                wait(act, back_ps, b - 1, NH, NH)
                nc.scalar.activation(gn[:, h, :], ga[:, h, :], ACT.Tanh, bias=col(V_BIH + 2)).then_inc(gn_ok, 1)

            nc.scalar.preload_act_table(ACT.Exp)
            act.wait_ge(w_in, 16)
            for n, (raw, dst) in enumerate(PIECES):
                if n == 1:
                    copy_xT(0, 0)
                    act.wait_ge(c2_in, 16)
                nc.scalar.activation(dst[:, 0], raw, ACT.Copy).then_inc(wH_ok, 1)
            act.wait_ge(prep_dve, N_PARAM)

            def step(b, q, first, last):
                relu_conv1(b, q)
                if not first:
                    candidate(b - 1, 1)
                embed(b)
                relu_msg(b)
                bn2(b, 0)
                exps(b)
                bn2(b, 1)
                if not last:
                    copy_xT(b + 1, 1 - q)
                else:
                    hi_of_x2T(0)
                gates(b, 0)
                candidate(b, 0)
                gates(b, 1)

            over_batches(act, step)

            def routing_weights(b, q):
                for h in range(NH):
                    wait(act, w_ps, b, NH, h + 1)
                    nc.scalar.activation(W[:, q, half(h)], Db[h][:, :], ACT.Identity,
                                         bias=col(V_BR)).then_inc(w_ok, 1)

            def gelu(b, u, first):
                h, j = divmod(u, HT)
                wait(act, f1_ps, b, NH * HT, u + 1)
                if j == 0:
                    wait(act, y_ps, b - 1, NH, h + 1)
                if u == 0:
                    wait(act, gL_ok, b - 1, NH * HT, NH * HT)
                nc.scalar.activation(g[:, h, j, :], up_bank(u, first)[:, :], ACT.Gelu_apprx_tanh,
                                     bias=col(V_F1 + j)).then_inc(g_ok, 1)
                wait(act, g_ok, b, NH * HT, u + 1)
                nc.scalar.activation(gH[h][j], g[:, h, j, :], ACT.Copy).then_inc(gH_ok, 1)

            def ffn_step(b, q, first, last):
                gelu(b, 0, first)
                if first:
                    candidate(B - 1, 1)
                routing_weights(b, q)
                for u in range(1, NH * HT):
                    gelu(b, u, first)
                if not last:
                    hi_of_x2T(b + 1)

            over_batches(act, ffn_step)

        @block.vector
        def _(dve):
            TS, TT, STT = nc.vector.tensor_scalar, nc.vector.tensor_tensor, nc.vector.scalar_tensor_tensor

            def moments(b, mean, ve, stats, mom1, mom2, agg):
                for t in range(T):
                    if isinstance(b, int) and b == 0 and stats is stats1 and t % TH == 0:
                        dve.wait_ge((x0_in, x_in[0])[t // TH], 16)
                    nc.vector.bn_stats(st[:, t, :], xall[:, b, t, :]).then_inc(stats, 1)
                (me, mo), (ve_, vo) = ((st[:, :, k], st[:, :, k + 3]) for k in (1, 2))
                wait(dve, stats, b, T, T)
                TT(msum[:, :], me, mo, ALU.add)
                TT(mdif[:, :], me, mo, ALU.subtract)
                TS(vsum[:, :], ve_, 1.0 / D, EPS, ALU.mult, ALU.add).then_inc(mom1, 1)
                wait(dve, mom1, b, 1, 1)
                TS(mean, msum[:, :], 0.5, None, ALU.mult)
                STT(mdif[:, :], mdif[:, :], 0.25, mdif[:, :], ALU.mult, ALU.mult)
                STT(vsum[:, :], vo, 1.0 / D, vsum[:, :], ALU.mult, ALU.add).then_inc(mom2, 1)
                wait(dve, mom2, b, 1, 1)
                TT(ve, vsum[:, :], mdif[:, :], ALU.add).then_inc(agg, 1)

            def moments1(b):
                moments(b, mean[:, :], ve[:, :], stats1, mom1, mom2, agg)

            def moments2(b):
                moments(b, mean2[:, b, :], ve2[:, :], st2, mo21, mo22, agg2)

            def normalise(b, mean, rstd, rstd_ok, ready):
                wait(dve, rstd_ok, b, 1, 1)
                for t in range(T):
                    i = TS(xn[:, t, :], xall[:, b, t, :], mean[:, t:t + 1], rstd[:, t:t + 1], ALU.subtract, ALU.mult)
                    if t % TH == TH - 1:
                        i.then_inc(ready, 1)

            moments1(0)
            normalise(0, mean[:, :], rstd[:, :], rstd_ok, xn_ok)
            dve.wait_ge(vec_in, 16)
            dve.wait_ge(prep_pool, 6)
            n_dve = 0

            def small(ins, chained=True):
                nonlocal n_dve
                ins.then_inc(prep_dve, 1)
                n_dve += 1
                if chained:
                    dve.wait_ge(prep_dve, n_dve)

            small(TT(col(V_SC1), col(V_G1), col(V_T1), ALU.mult), False)
            small(TT(col(V_SC2), col(V_G2), col(V_T2), ALU.mult))
            small(TT(col(V_T1), col(V_M1), col(V_SC1), ALU.mult), False)
            small(TT(col(V_T2), col(V_M2), col(V_SC2), ALU.mult))
            small(TT(col(V_SH1), col(V_B1), col(V_T1), ALU.subtract), False)
            small(TT(col(V_SH2), col(V_B2), col(V_T2), ALU.subtract), False)
            small(TT(col(V_GB, 2), col(V_BIH, 2), col(V_BHH, 2), ALU.add))
            small(TS(col(V_GB, 2), col(V_GB, 2), 0.5, None, ALU.mult), False)
            small(TS(col(V_NHB), col(V_BHH + 2), 0.5, None, ALU.mult), False)
            assert n_dve == N_PARAM

            def lo_of_weights(n):
                raw, dst = PIECES[n]
                dve.wait_ge(wH_ok, n + 1)
                TT(dst[:, 1], raw, f32(dst[:, 0]), ALU.subtract).then_inc(wL_ok, 1)

            lo_of_weights(0)

            def zero_pads():
                for hb in (hH, hL):
                    nc.vector.memset(f32(hb[:, 0:PAD]), 0.0)
                    i = nc.vector.memset(f32(hb[:, PAD + N:]), 0.0)
                i.then_inc(prep_dve, 1)

            zero_pads()

            def split_xT(b, q):
                for h in range(NH):
                    wait(dve, xT_ok, b, NH, h + 1)
                    nc.vector.tensor_copy(xTH[:, q, half(h)], xT[:, q, half(h)]).then_inc(xTH_ok, 1)
                    wait(dve, xTH_ok, b, NH, h + 1)
                    TT(xTL[:, q, half(h)], xT[:, q, half(h)], f32(xTH[:, q, half(h)]),
                       ALU.subtract).then_inc(xTL_ok, 1)

            def split_h(b):
                for h in range(NH):
                    hs = slice(PAD + h * HALF, PAD + (h + 1) * HALF)
                    wait(dve, h_ok, b, NH, h + 1)
                    if h == 0:
                        wait(dve, c2_ps, b - 1, NH, NH)
                    nc.vector.tensor_copy(hH[:, hs], wk[:, half(h)]).then_inc(hH_ok, 1)
                    wait(dve, hH_ok, b, NH, h + 1)
                    TT(hL[:, hs], wk[:, half(h)], f32(hH[:, hs]), ALU.subtract).then_inc(hL_ok, 1)

            def new_gate(b, h):
                ni = D0 if h == 0 else N0
                wait(dve, tr_ok, b, NH, h + 1)
                STT(ga[:, h, :], tr[:, h, :], 1.0, ga[:, h, :], ALU.add, ALU.mult).then_inc(q1_ok, 1)
                wait(dve, q1_ok, b, NH, h + 1)
                wait(dve, gate_ps, b, 8, 4 * h + 4)
                TT(ga[:, h, :], ga[:, h, :], ni[:, :], ALU.add).then_inc(q2_ok, 1)

            def blend(b, h, q):
                wait(dve, gn_ok, b, NH, h + 1)
                TT(ga[:, h, :], xT[:, q, half(h)], gn[:, h, :], ALU.subtract).then_inc(d_ok, 1)
                wait(dve, d_ok, b, NH, h + 1)
                wait(dve, tz_ok, b, NH, h + 1)
                STT(ga[:, h, :], tz[:, h, :], 1.0, ga[:, h, :], ALU.add, ALU.mult).then_inc(e_ok, 1)
                wait(dve, e_ok, b, NH, h + 1)
                STT(gn[:, h, :], ga[:, h, :], 0.5, gn[:, h, :], ALU.mult, ALU.add).then_inc(o_ok, 1)

            def add_msg_bias(b):
                for h in range(NH):
                    wait(dve, m_ps, b, NH, h + 1)
                    if h == 0:
                        wait(dve, nm_ps, b - 1, NU, NU)
                    TT(msg[:, h * TH:(h + 1) * TH, :], Db[h][:, :].rearrange("p (t d) -> p t d", t=TH),
                       bmsg.unsqueeze(1).broadcast_to([P, TH, D]), ALU.add).then_inc(mb_ok, 1)

            def distance_operands(b):
                for h in range(NH):
                    hs = half(h)
                    wait(dve, s_ok, b, 2 * NH, 2 * h + 2)
                    if h == 0:
                        wait(dve, d_ps, b - 1, NU, NU)
                    nc.vector.tensor_copy(sH[:, hs], wk[:, hs]).then_inc(sH_ok, 1)
                    wait(dve, sH_ok, b, NH, h + 1)
                    TT(sL[:, hs], wk[:, hs], f32(sH[:, hs]), ALU.subtract).then_inc(sL_ok, 1)
                    TS(U[:, hs], f32(sH[:, hs]), mask(U_HI), mask(U_ONE), ALU.mult, ALU.add).then_inc(UV0_ok, 1)
                    TS(V[:, hs], f32(sH[:, hs]), mask(V_HI), mask(V_ONE), ALU.mult, ALU.add).then_inc(UV0_ok, 1)
                    wait(dve, sL_ok, b, NH, h + 1)
                    wait(dve, UV0_ok, b, 2 * NH, 2 * h + 2)
                    STT(U[:, hs], f32(sL[:, hs]), mask(U_LO), f32(U[:, hs]), ALU.mult, ALU.add).then_inc(UV_ok, 1)
                    STT(V[:, hs], f32(sL[:, hs]), mask(V_LO), f32(V[:, hs]), ALU.mult, ALU.add).then_inc(UV_ok, 1)

            def state_to_nodes(b):
                for h in range(NH):
                    wait(dve, back_ps, b, NH, h + 1)
                    xs = xall[:, b, h * TH:(h + 1) * TH, :]
                    TT(xs, xs, Nb[h][:, :].rearrange("p (t d) -> p t d", t=TH), ALU.add).then_inc(x1_ok, 1)

            def split_msg(b):
                for h in range(NH):
                    ts = slice(h * TH, (h + 1) * TH)
                    wait(dve, msg_ok, b, NH, h + 1)
                    nc.vector.tensor_copy(msgH[:, ts, :], msg[:, ts, :]).then_inc(msgH_ok, 1)
                    wait(dve, msgH_ok, b, NH, h + 1)
                    TT(msgL[:, ts, :], msg[:, ts, :], f32(msgH[:, ts, :]), ALU.subtract).then_inc(msgL_ok, 1)

            def conv_out(b, h, q):
                hs = half(h)
                wait(dve, c2_ok, b, NH, h + 1)
                TT(wk[:, hs], wk[:, hs], xT[:, q, hs], ALU.add).then_inc(pre_ok, 1)
                wait(dve, pre_ok, b, NH, h + 1)
                TS(xcH[:, hs], wk[:, hs], 0.0, None, ALU.max).then_inc(xcH_ok, 1)
                wait(dve, xcH_ok, b, NH, h + 1)
                STT(xcL[:, hs], wk[:, hs], 0.0, f32(xcH[:, hs]), ALU.max, ALU.subtract).then_inc(xcL_ok, 1)

            def weigh(b, u):
                wait(dve, exp_ok, b, NU, u + 1)
                wait(dve, k_ps, b, NU, u + 1)
                wait(dve, AH_ok, b, NU, u + 1 - NA)
                TT(A[u % NA], E[:, u % NE, :], Mb[u % NH][:, :], ALU.mult).then_inc(A_ok, 1)

            def lo_of_adjacency(b, v):
                wait(dve, AH_ok, b, NU, v + 1)
                wait(dve, nm_ps, b, NU, v + 1 - NS)
                TT(AL[:, v % NS, :], A[v % NA], f32(AH[:, v % NS, :]), ALU.subtract).then_inc(AL_ok, 1)

            def split_nmp(b):
                for h in range(NH):
                    wait(dve, nm_ps, b, NU, NU - NH + h + 1)
                    nc.vector.tensor_copy(nmH[:, half(h)], Nb[h][:, :]).then_inc(nmH_ok, 1)
                    wait(dve, nmH_ok, b, NH, h + 1)
                    TT(nmL[:, half(h)], Nb[h][:, :], f32(nmH[:, half(h)]), ALU.subtract).then_inc(nmL_ok, 1)

            def prepare(b):
                if not (isinstance(b, int) and b == 0):
                    wait(dve, base_ok, b - 1, 1, 1)
                    wait(dve, t2_ps, b - 1, NH, NH)
                normalise(b, mean2[:, b, :], rstd2[:, b, :], rstd2_ok, xn2_ok)

            def lo_of_x2T(b):
                for h in range(NH):
                    wait(dve, t2H_ok, b, NH, h + 1)
                    TT(xTL[:, 0, half(h)], Db[h][:, :], f32(xTH[:, 0, half(h)]), ALU.subtract).then_inc(t2L_ok, 1)

            split_xT(0, 0)
            lo_of_weights(1)

            def step(b, q, first, last):
                split_h(b)
                if not first:
                    new_gate(b - 1, 1)
                add_msg_bias(b)
                if first:
                    lo_of_weights(2)
                else:
                    blend(b - 1, 1, 1 - q)
                distance_operands(b)
                if not last:
                    dve.wait_ge(x_in[1 - q], (b + q) * 8 + 16)
                    moments1(b + 1)
                if not first:
                    state_to_nodes(b - 1)
                split_msg(b)
                if not last:
                    normalise(b + 1, mean[:, :], rstd[:, :], rstd_ok, xn_ok)
                else:
                    prepare(0)
                conv_out(b, 0, q)
                for u in range(NU + 1):
                    if u < NU:
                        weigh(b, u)
                    if u > 0:
                        lo_of_adjacency(b, u - 1)
                split_nmp(b)
                if not last:
                    conv_out(b, 1, q)
                    split_xT(b + 1, 1 - q)
                else:
                    lo_of_x2T(0)
                    conv_out(b, 1, q)
                if not first:
                    wait(dve, x1_ok, b - 1, NH, NH)
                if last:
                    dve.wait_ge(rstd2_ok, B - 2)
                new_gate(b, 0)
                blend(b, 0, q)
                if not first:
                    moments2(b - 1)

            over_batches(dve, step)
            new_gate(B - 1, 1)
            blend(B - 1, 1, (B - 1) % 2)
            state_to_nodes(B - 1)
            dve.wait_ge(x1_ok, NH * B)

            def rank_columns(b, q):
                wait(dve, wc_ps, b, 2, 2)
                for h in range(NH):
                    i = nc.vector.tensor_copy(wcol[:, q, h * TH:(h + 1) * TH], Db[h][:, 0:TH * ROWS]
                                              .rearrange("p (t c) -> p t c", t=TH)[:, :, 0])
                i.then_inc(wc_ok, 1)
                wait(dve, wc_ok, b, 1, 1)

            def compare(b, q, t):
                w = wcol[:, q, t:t + 1]
                wait(dve, cnt_ps, b, T, t + 1 - NC)
                i = TS(Cmp[t % NC][:, 0:(t + 1) * P], W[:, q, 0:(t + 1) * P], w, None, ALU.is_lt)
                if t < T - 1:
                    i = TS(Cmp[t % NC][:, (t + 1) * P:], W[:, q, (t + 1) * P:], w, None, ALU.is_le)
                STT(Eq[t % NC], W[:, q, t * P:(t + 1) * P], w, tri, ALU.is_equal, ALU.mult).then_inc(cmp_ok, 1)

            def select(b, q):
                for h in range(NH):
                    hs = half(h)
                    wait(dve, cnt_ps, b, T, T)
                    STT(ws[:, hs], Mb[h][:, :], float(KEEP), W[:, q, hs], ALU.is_lt, ALU.mult).then_inc(ws_ok, 1)
                    wait(dve, ws_ok, b, NH, h + 1)
                    wait(dve, y_ps, b, NH, h + 1)
                    STT(gn[:, h, :], Nb[h][:, :], col(V_F2), ws[:, hs], ALU.add, ALU.mult).then_inc(ys_ok, 1)

            def finish(b):
                for h in range(NH):
                    wait(dve, fb_ps, b, NH, h + 1)
                    wait(dve, base_ok, b, 1, 1)
                    xs = xall[:, b, h * TH:(h + 1) * TH, :]
                    TT(xs, xs, Mb[h][:, :].rearrange("p (t d) -> p t d", t=TH), ALU.add).then_inc(fin_ok, 1)

            def ffn_step(b, q, first, last):
                if not first:
                    select(b - 1, 1 - q)
                    finish(b - 1)
                rank_columns(b, q)
                for t in range(T):
                    if first and t == 2:
                        dve.wait_ge(rstd2_ok, B - 1)
                        moments2(B - 1)
                    if t == T // 2 and not last:
                        prepare(b + 1)
                    compare(b, q, t)
                if not last:
                    lo_of_x2T(b + 1)

            over_batches(dve, ffn_step)
            select(B - 1, (B - 1) % 2)
            finish(B - 1)

        @block.tensor
        def _(pe):
            MM, TR = nc.tensor.matmul, nc.tensor.transpose

            def three(out_, wgt, hi, lo, start, stop):
                MM(out_, wgt(0), hi, start=start, stop=False)
                MM(out_, wgt(0), lo, start=False, stop=False)
                return MM(out_, wgt(1), hi, start=False, stop=stop)

            def nodes_to_features(b, ready, s):
                for h in range(NH):
                    wait(pe, ready, b, NH, h + 1)
                    for k in range(TH):
                        i = TR(Db[h][:, k * P:(k + 1) * P], xn[:, h * TH + k, :], ident)
                    i.then_inc(s, 1)

            def conv1(b, q):
                wait(pe, q2_ok, b - 1, NH, 1)
                for h in range(NH):
                    wait(pe, xTL_ok, b, NH, h + 1)
                    three(Db[h][:, :], weight(W_C1), xTH[:, q, half(h)], xTL[:, q, half(h)],
                          True, True).then_inc(c1_ps, 1)

            def embedding(b, q):
                wait(pe, tz_ok, b - 1, NH, 1)
                for h in range(NH):
                    three(Mb[h][:, :], weight(W_SE), xTH[:, q, half(h)], xTL[:, q, half(h)],
                          True, True).then_inc(s_ps, 1)

            def messages(b, q):
                for h in range(NH):
                    wait(pe, h_ok, b, NH, h + 1)
                    for k in range(TH):
                        o_ = Db[h][:, k * P:(k + 1) * P]
                        xh, xl = xTH[:, q, tile(h, k)], xTL[:, q, tile(h, k)]
                        MM(o_, xh, weight(W_MSG)(0), start=True, stop=False)
                        MM(o_, xh, weight(W_MSG)(1), start=False, stop=False)
                        i = MM(o_, xl, weight(W_MSG)(0), start=False, stop=True)
                    i.then_inc(m_ps, 1)

            def conv2(b, h):
                if isinstance(b, int) and b == 0:
                    pe.wait_ge(wL_ok, 2)
                wait(pe, hL_ok, b, NH, NH)
                if h == 0:
                    wait(pe, tz_ok, b - 1, NH, 2)
                for k in range(K2):
                    if h == 1 and k in EARLY:
                        front(b, EARLY[k])
                    a = slice(h * HALF + k, h * HALF + k + HALF)
                    i = three(Cb[h][:, :], lambda w: wc2[:, w, k * D:(k + 1) * D], hH[:, a], hL[:, a], k == 0, k == K2 - 1)
                i.then_inc(c2_ps, 1)

            def state_back(b):
                for h in range(NH):
                    wait(pe, o_ok, b, NH, NH)
                    for k in range(TH):
                        i = TR(Nb[h][:, k * P:(k + 1) * P], gn[:, h, k * P:(k + 1) * P], ident)
                    i.then_inc(back_ps, 1)

            def front(b, u):
                t, h = divmod(u, NH)
                if u == 0:
                    wait(pe, UV_ok, b, 2 * NH, 2 * NH)
                    wait(pe, adj_in, b, 16, 16)
                    wait(pe, msgL_ok, b, NH, NH)
                    wait(pe, s_ok, b, 2 * NH, 2 * NH)
                if u >= NH:
                    wait(pe, exp_ok, b, NU, u + 1 - NH)
                MM(Db[h][:, :], U[:, t * P:(t + 1) * P], V[:, half(h)], start=True, stop=True).then_inc(d_ps, 1)
                if u >= NH:
                    wait(pe, A_ok, b, NU, u + 1 - NH)
                for k in range(TH):
                    i = TR(Mb[h][:, k * P:(k + 1) * P], adjb[:, h * TH + k, t * P:(t + 1) * P], ident)
                i.then_inc(k_ps, 1)

            def adjacency(b, last):
                wait(pe, x1_ok, b - 1, NH, NH)
                for u in range(LAG, NU + LAG):
                    if u < NU:
                        front(b, u)
                    if u == NU + 1:
                        wait(pe, exp_ok, b, NU, NU)
                        if not last:
                            nodes_to_features(b + 1, xn_ok, xT_ps)
                        else:
                            x2_to_features(0)
                    v = u - LAG
                    t, h = divmod(v, NH)
                    wait(pe, AL_ok, b, NU, v + 1)
                    three(Nb[h][:, :], lambda k: (msgH, msgL)[k][:, t, :], AH[:, v % NS, :],
                          AL[:, v % NS, :], t == 0, t == T - 1).then_inc(nm_ps, 1)

            def gru(b, h, q):
                r, z, ni, nh = (M0, M1, D0, D1) if h == 0 else (C0, C1, N0, N1)
                hs = half(h)
                X = (xTH[:, q, hs], xTL[:, q, hs])
                XC = (xcH[:, hs], xcL[:, hs])
                NM = (nmH[:, hs], nmL[:, hs])

                def wi(gate, part):
                    return weight(W_IH + (2 * gate + part) * D)

                def wh(gate):
                    return weight(W_HH + gate * D)

                if isinstance(b, int) and b == 0:
                    pe.wait_ge(wL_ok, len(PIECES))
                if h == 0:
                    wait(pe, A_ok, b, NU, NU)
                wait(pe, xcL_ok, b, NH, h + 1)
                three(r[:, :], wh(0), *X, True, False)
                three(r[:, :], wi(0, 0), *XC, False, False)
                three(z[:, :], wh(1), *X, True, False)
                three(z[:, :], wi(1, 0), *XC, False, False)
                return r, z, ni, nh, X, XC, NM, wi, wh

            def gru_rest(b, h, q, parts, last):
                r, z, ni, nh, X, XC, NM, wi, wh = parts
                if h == 0:
                    if not last:
                        wait(pe, xT_ok, b + 1, NH, NH)
                    else:
                        wait(pe, t2L_ok, 0, NH, NH)
                else:
                    wait(pe, nmL_ok, b, NH, NH)
                three(nh[:, :], wh(2), *X, True, True).then_inc(gate_ps, 1)
                three(ni[:, :], wi(2, 0), *XC, True, False)
                wait(pe, nmL_ok, b, NH, h + 1)
                three(r[:, :], wi(0, 1), *NM, False, True).then_inc(gate_ps, 1)
                three(z[:, :], wi(1, 1), *NM, False, True).then_inc(gate_ps, 1)
                three(ni[:, :], wi(2, 1), *NM, False, True).then_inc(gate_ps, 1)

            def x2_to_features(b):
                nodes_to_features(b, xn2_ok, t2_ps)

            pe.wait_ge(cst_in, 16)
            nodes_to_features(0, xn_ok, xT_ps)
            pe.wait_ge(wL_ok, 1)

            def step(b, q, first, last):
                conv1(b, q)
                embedding(b, q)
                messages(b, q)
                conv2(b, 0)
                if not first:
                    state_back(b - 1)
                conv2(b, 1)
                adjacency(b, last)
                for h in range(NH):
                    gru_rest(b, h, q, gru(b, h, q), last)

            over_batches(pe, step)

            def ffn_up(b, us, first):
                for u in us:
                    h, j = divmod(u, HT)
                    if not (first and u < 4):
                        wait(pe, g_ok, b, NH * HT, u - 1)
                    three(up_bank(u, first)[:, :], weight(W_F1 + j * D), xTH[:, 0, half(h)],
                          xTL[:, 0, half(h)], True, True).then_inc(f1_ps, 1)

            def ffn_down(b, h, j):
                wait(pe, gL_ok, b, NH * HT, h * HT + j + 1)
                i = three(Nb[h][:, :], weight(W_F2 + j * D), gH[h][j], gL[h][j], j == 0, j == HT - 1)
                if j == HT - 1:
                    i.then_inc(y_ps, 1)

            def weight_columns(b, q):
                for h in range(NH):
                    for k in range(TH):
                        i = TR(Db[h][:, k * ROWS:(k + 1) * ROWS], W[0:ROWS, q, tile(h, k)],
                               ident[0:ROWS, 0:ROWS])
                    i.then_inc(wc_ps, 1)

            def count(b, t):
                wait(pe, cmp_ok, b, T, t + 1)
                e = t // TH
                for h in range(NH):
                    MM(Mb[h][:, :], ones[:, :], Cmp[t % NC][:, half(h)], start=(t == 0),
                       stop=(t == T - 1 and h != e))
                MM(Mb[e][:, (t % TH) * P:(t % TH + 1) * P], ones[:, :], Eq[t % NC], start=False,
                   stop=(t == T - 1)).then_inc(cnt_ps, 1)

            def update_back(b):
                for h in range(NH):
                    wait(pe, ys_ok, b, NH, h + 1)
                    for k in range(TH):
                        i = TR(Mb[h][:, k * P:(k + 1) * P], gn[:, h, k * P:(k + 1) * P], ident)
                    i.then_inc(fb_ps, 1)

            def routing(b, first):
                if first:
                    pe.wait_ge(q2_ok, NH * (B - 1) + 1)
                for h in range(NH):
                    three(Db[h][:, :], weight(W_R), xTH[:, 0, half(h)], xTL[:, 0, half(h)],
                          True, True).then_inc(w_ps, 1)

            def ffn_step(b, q, first, last):
                wait(pe, t2L_ok, b, NH, 1)
                if first:
                    pe.wait_ge(tz_ok, NH * (B - 1) + 1)
                ffn_up(b, (0, 1), first)
                wait(pe, t2L_ok, b, NH, NH)
                routing(b, first)
                if first:
                    pe.wait_ge(tz_ok, NH * B)
                    ffn_up(b, (2, 3), first)
                    pe.wait_ge(w_ok, NH)
                    weight_columns(b, q)
                    state_back(B - 1)
                    pe.wait_ge(g_ok, 2)
                    pe.wait_ge(x1_ok, NH * B)
                else:
                    update_back(b - 1)
                    wait(pe, w_ok, b, NH, NH)
                    ffn_up(b, (2,), first)
                    weight_columns(b, q)
                    ffn_up(b, (3,), first)
                ffn_up(b, (4,), first)
                if not first:
                    wait(pe, fin_ok, b - 1, NH, NH)
                for u in range(NH * HT):
                    if u == T - 1:
                        count(b, u - 1)
                        count(b, u)
                    ffn_down(b, *divmod(u, HT))
                    if u == T - 2 and not last:
                        wait(pe, wc_ok, b, 1, 1)
                        x2_to_features(b + 1)
                    if 0 < u < T - 1:
                        count(b, u - 1)
                    if u + HT + 1 < NH * HT:
                        ffn_up(b, (u + HT + 1,), first)

            over_batches(pe, ffn_step)
            update_back(B - 1)


def kernel(**inputs):
    import concourse.bacc as _bacc
    from concourse.bass_utils import run_bass_kernel_spmd as _run

    nc = _bacc.Bacc("TRN2", target_bir_lowering=False, num_devices=1)
    arrays, args = {}, []
    vectors, weights, conv2_w = lay_out(inputs)
    given = {"x": inputs["x"], "adj": inputs["adj"], "vectors": vectors, "weights": weights,
             "conv2_w": conv2_w, "const": constants()}
    for name, a in given.items():
        a = np.ascontiguousarray(a)
        arrays[f"in_{name}"] = a
        args.append(nc.dram_tensor(f"in_{name}", a.shape, mybir.dt.from_np(a.dtype), kind="ExternalInput").ap())
    args.append(nc.dram_tensor("out_0", (B, N, D), F32, kind="ExternalOutput").ap())
    build(nc, *args)
    r = _run(nc, [arrays], core_ids=[0])
    return r.results[0]["out_0"]
```
